# Optimizing a Trainium2 kernel written in Bass

```python
import numpy as np
import jax
import jax.numpy as jnp

def _softmax(x, axis=-1):
    return jax.nn.softmax(x, axis=axis)

def _gelu(x):
    return jax.nn.gelu(x, approximate=True)

def _silu(x):
    return jax.nn.silu(x)

def _sigmoid(x):
    return jax.nn.sigmoid(x)

def _layernorm(x, axis=-1, eps=1e-05):
    m = jnp.mean(x, axis=axis, keepdims=True)
    v = jnp.var(x, axis=axis, keepdims=True)
    return (x - m) / jnp.sqrt(v + eps)

def _scatter_add(tgt, idx, src, axis=0):
    return tgt.at[idx].add(src)

def _segment_sum(src, seg, n):
    return jax.ops.segment_sum(src, seg, n)
kernel_name = 'mk_xattn_ffn_d1_seqx_r8_363d4e'

def setup_inputs(seed: int=0):
    np.random.seed(seed)
    _w = jnp.asarray

    def _rec_inputs():
        import jax
        import jax.numpy as jnp
        _rk = jax.random.key(seed)
        x = -0.0002928 + 1 * jax.random.normal(jax.random.fold_in(_rk, 1), (8, 128, 128), jnp.float32)
        _lenS = 128 - jax.random.randint(jax.random.fold_in(_rk, 7), (8,), 0, max(1, 128 // 4) + 1, jnp.int32)
        _lenS2 = 128 - jax.random.randint(jax.random.fold_in(_rk, 8), (8,), 0, max(1, 128 // 4) + 1, jnp.int32)
        _ctx_1024P = jax.random.normal(jax.random.fold_in(_rk, 11), (8, 16, 128), jnp.float32)
        _ctx_1024c = jax.random.dirichlet(jax.random.fold_in(_rk, 511), 0.3 * jnp.ones((16,), jnp.float32), (8, 128))
        _ctx_1024t = jnp.einsum('bsk,bkd->bsd', _ctx_1024c, _ctx_1024P)
        _ctx_1024t = _ctx_1024t * jax.lax.rsqrt(jnp.mean(jnp.square(_ctx_1024t)) + 1e-12) * 0.953939
        ctx_1024 = -1.39393e-06 + 0.999914 * (_ctx_1024t + 0.3 * jax.random.normal(jax.random.fold_in(_rk, 611), (8, 128, 128), jnp.float32))
        return (x, ctx_1024)
    x, ctx_1024 = _rec_inputs()

    def _L0_xattn_setup():
        import jax, jax.numpy as jnp
        import numpy as np
        D_MODEL = 128
        NUM_HEADS = 16
        D_K = D_MODEL // NUM_HEADS

        def _split_heads(x):
            B, S, _ = x.shape
            return x.reshape(B, S, NUM_HEADS, D_K).transpose(0, 2, 1, 3)
        key = jax.random.key(seed)
        ks = jax.random.split(key, 12)
        B, S = (2, 256)
        s = 1.0 / np.sqrt(D_MODEL)
        inp = {'query': jax.random.normal(ks[0], (B, S, D_MODEL), jnp.float32), 'key': jax.random.normal(ks[1], (B, S, D_MODEL), jnp.float32), 'value': jax.random.normal(ks[2], (B, S, D_MODEL), jnp.float32), 'Wq': jax.random.normal(ks[3], (D_MODEL, D_MODEL), jnp.float32) * s, 'bq': jax.random.normal(ks[4], (D_MODEL,), jnp.float32) * s, 'Wk': jax.random.normal(ks[5], (D_MODEL, D_MODEL), jnp.float32) * s, 'bk': jax.random.normal(ks[6], (D_MODEL,), jnp.float32) * s, 'Wv': jax.random.normal(ks[7], (D_MODEL, D_MODEL), jnp.float32) * s, 'bv': jax.random.normal(ks[8], (D_MODEL,), jnp.float32) * s, 'Wo': jax.random.normal(ks[9], (D_MODEL, D_MODEL), jnp.float32) * s, 'bo': jax.random.normal(ks[10], (D_MODEL,), jnp.float32) * s}
        return inp
    _L0_xattn_all = _L0_xattn_setup()
    _L0_xattn_in = {k: v for k, v in _L0_xattn_all.items() if k in ('Wq', 'bq', 'Wk', 'bk', 'Wv', 'bv', 'Wo', 'bo')}
    del _L0_xattn_all

    def _L0_ffn_setup():
        import jax, jax.numpy as jnp
        import numpy as np
        D = 128
        H = 16
        FF = 512
        E = 8
        K = 2
        EH = 128
        B, S = (2, 256)
        EPS = 1e-05

        def rmsnorm(x, w):
            v = jnp.mean(jnp.square(x), axis=-1, keepdims=True)
            return x * jax.lax.rsqrt(v + EPS) * w

        def _dense_path(x, wq, wk, wv, wo, w1, w2, w3, attn_norm_w, ff_norm_w):
            b, s, d = x.shape
            hd = d // H
            q = (x @ wq).reshape(b, s, H, hd)
            k = (x @ wk).reshape(b, s, H, hd)
            v = (x @ wv).reshape(b, s, H, hd)
            scores = jnp.einsum('bqhd,bkhd->bhqk', q, k) / np.sqrt(hd).astype(np.float32)
            causal = jnp.tril(jnp.ones((s, s), bool))
            scores = jnp.where(causal, scores, jnp.finfo(scores.dtype).min)
            attn = jax.nn.softmax(scores, axis=-1)
            o = jnp.einsum('bhqk,bkhd->bqhd', attn, v).reshape(b, s, d)
            h = x + rmsnorm(o @ wo, attn_norm_w)
            ffn = jax.nn.silu(h @ w1) * (h @ w3) @ w2
            return h + rmsnorm(ffn, ff_norm_w)

        def _sparse_path(x, router_w, ew1, ew2, ew3, moe_norm_w):
            b, s, d = x.shape
            xt = x.reshape(-1, d)
            probs = jax.nn.softmax(xt @ router_w, axis=-1)
            topw, topi = jax.lax.top_k(probs, K)
            g = jax.nn.silu(jnp.einsum('td,edh->eth', xt, ew1)) * jnp.einsum('td,edh->eth', xt, ew3)
            eo = jnp.einsum('eth,ehd->ted', g, ew2)
            sel = jnp.take_along_axis(eo, topi[:, :, None], axis=1)
            moe_out = jnp.sum(topw[:, :, None] * sel, axis=1).reshape(b, s, d)
            return rmsnorm(moe_out, moe_norm_w)
        key = jax.random.key(seed)
        ks = jax.random.split(key, 16)
        s = 0.02
        return {'x': jax.random.normal(ks[0], (B, S, D), jnp.float32), 'wq': jax.random.normal(ks[1], (D, D), jnp.float32) * s, 'wk': jax.random.normal(ks[2], (D, D), jnp.float32) * s, 'wv': jax.random.normal(ks[3], (D, D), jnp.float32) * s, 'wo': jax.random.normal(ks[4], (D, D), jnp.float32) * s, 'w1': jax.random.normal(ks[5], (D, FF), jnp.float32) * s, 'w2': jax.random.normal(ks[6], (FF, D), jnp.float32) * s, 'w3': jax.random.normal(ks[7], (D, FF), jnp.float32) * s, 'attn_norm_w': jnp.ones((D,), jnp.float32), 'ff_norm_w': jnp.ones((D,), jnp.float32), 'moe_norm_w': jnp.ones((D,), jnp.float32), 'router_w': jax.random.normal(ks[8], (D, E), jnp.float32) * s, 'ew1': jax.random.normal(ks[9], (E, D, EH), jnp.float32) * s, 'ew2': jax.random.normal(ks[10], (E, EH, D), jnp.float32) * s, 'ew3': jax.random.normal(ks[11], (E, D, EH), jnp.float32) * s}
    _L0_ffn_all = _L0_ffn_setup()
    _L0_ffn_in = {k: v for k, v in _L0_ffn_all.items() if k in ('wq', 'wk', 'wv', 'wo', 'w1', 'w2', 'w3', 'attn_norm_w', 'ff_norm_w', 'moe_norm_w', 'router_w', 'ew1', 'ew2', 'ew3')}
    del _L0_ffn_all
    return {'x': x, 'ctx_1024': ctx_1024, 'L0_xattn_Wq': _L0_xattn_in['Wq'], 'L0_xattn_bq': _L0_xattn_in['bq'], 'L0_xattn_Wk': _L0_xattn_in['Wk'], 'L0_xattn_bk': _L0_xattn_in['bk'], 'L0_xattn_Wv': _L0_xattn_in['Wv'], 'L0_xattn_bv': _L0_xattn_in['bv'], 'L0_xattn_Wo': _L0_xattn_in['Wo'], 'L0_xattn_bo': _L0_xattn_in['bo'], 'L0_ffn_wq': _L0_ffn_in['wq'], 'L0_ffn_wk': _L0_ffn_in['wk'], 'L0_ffn_wv': _L0_ffn_in['wv'], 'L0_ffn_wo': _L0_ffn_in['wo'], 'L0_ffn_w1': _L0_ffn_in['w1'], 'L0_ffn_w2': _L0_ffn_in['w2'], 'L0_ffn_w3': _L0_ffn_in['w3'], 'L0_ffn_attn_norm_w': _L0_ffn_in['attn_norm_w'], 'L0_ffn_ff_norm_w': _L0_ffn_in['ff_norm_w'], 'L0_ffn_moe_norm_w': _L0_ffn_in['moe_norm_w'], 'L0_ffn_router_w': _L0_ffn_in['router_w'], 'L0_ffn_ew1': _L0_ffn_in['ew1'], 'L0_ffn_ew2': _L0_ffn_in['ew2'], 'L0_ffn_ew3': _L0_ffn_in['ew3']}

def reference(x, ctx_1024, L0_xattn_Wq, L0_xattn_bq, L0_xattn_Wk, L0_xattn_bk, L0_xattn_Wv, L0_xattn_bv, L0_xattn_Wo, L0_xattn_bo, L0_ffn_wq, L0_ffn_wk, L0_ffn_wv, L0_ffn_wo, L0_ffn_w1, L0_ffn_w2, L0_ffn_w3, L0_ffn_attn_norm_w, L0_ffn_ff_norm_w, L0_ffn_moe_norm_w, L0_ffn_router_w, L0_ffn_ew1, L0_ffn_ew2, L0_ffn_ew3):
    import jax
    import jax.numpy as jnp

    def _L0_xattn_ref(query, key, value, Wq, bq, Wk, bk, Wv, bv, Wo, bo):
        import jax, jax.numpy as jnp
        import numpy as np
        D_MODEL = 128
        NUM_HEADS = 16
        D_K = D_MODEL // NUM_HEADS

        def _split_heads(x):
            B, S, _ = x.shape
            return x.reshape(B, S, NUM_HEADS, D_K).transpose(0, 2, 1, 3)
        Q = _split_heads(query @ Wq.T + bq)
        K = _split_heads(key @ Wk.T + bk)
        V = _split_heads(value @ Wv.T + bv)
        scale = 1.0 / jnp.sqrt(jnp.asarray(D_K, Q.dtype))
        scores = jnp.einsum('bhqd,bhkd->bhqk', Q, K) * scale
        attn = jax.nn.softmax(scores, axis=-1)
        x = jnp.einsum('bhqk,bhkd->bhqd', attn, V)
        B, H, S, Dk = x.shape
        x = x.transpose(0, 2, 1, 3).reshape(B, S, H * Dk)
        return x @ Wo.T + bo

    def _L0_ffn_ref(x, wq, wk, wv, wo, w1, w2, w3, attn_norm_w, ff_norm_w, moe_norm_w, router_w, ew1, ew2, ew3):
        import jax, jax.numpy as jnp
        import numpy as np
        D = 128
        H = 16
        FF = 512
        E = 8
        K = 2
        EH = 128
        B, S = (2, 256)
        EPS = 1e-05

        def rmsnorm(x, w):
            v = jnp.mean(jnp.square(x), axis=-1, keepdims=True)
            return x * jax.lax.rsqrt(v + EPS) * w

        def _dense_path(x, wq, wk, wv, wo, w1, w2, w3, attn_norm_w, ff_norm_w):
            b, s, d = x.shape
            hd = d // H
            q = (x @ wq).reshape(b, s, H, hd)
            k = (x @ wk).reshape(b, s, H, hd)
            v = (x @ wv).reshape(b, s, H, hd)
            scores = jnp.einsum('bqhd,bkhd->bhqk', q, k) / np.sqrt(hd).astype(np.float32)
            causal = jnp.tril(jnp.ones((s, s), bool))
            scores = jnp.where(causal, scores, jnp.finfo(scores.dtype).min)
            attn = jax.nn.softmax(scores, axis=-1)
            o = jnp.einsum('bhqk,bkhd->bqhd', attn, v).reshape(b, s, d)
            h = x + rmsnorm(o @ wo, attn_norm_w)
            ffn = jax.nn.silu(h @ w1) * (h @ w3) @ w2
            return h + rmsnorm(ffn, ff_norm_w)

        def _sparse_path(x, router_w, ew1, ew2, ew3, moe_norm_w):
            b, s, d = x.shape
            xt = x.reshape(-1, d)
            probs = jax.nn.softmax(xt @ router_w, axis=-1)
            topw, topi = jax.lax.top_k(probs, K)
            g = jax.nn.silu(jnp.einsum('td,edh->eth', xt, ew1)) * jnp.einsum('td,edh->eth', xt, ew3)
            eo = jnp.einsum('eth,ehd->ted', g, ew2)
            sel = jnp.take_along_axis(eo, topi[:, :, None], axis=1)
            moe_out = jnp.sum(topw[:, :, None] * sel, axis=1).reshape(b, s, d)
            return rmsnorm(moe_out, moe_norm_w)
        dense_out = _dense_path(x, wq, wk, wv, wo, w1, w2, w3, attn_norm_w, ff_norm_w)
        sparse_out = _sparse_path(x, router_w, ew1, ew2, ew3, moe_norm_w)
        return dense_out + sparse_out
    x = x + _L0_xattn_ref(_layernorm(x, axis=-1), ctx_1024, ctx_1024, L0_xattn_Wq, L0_xattn_bq, L0_xattn_Wk, L0_xattn_bk, L0_xattn_Wv, L0_xattn_bv, L0_xattn_Wo, L0_xattn_bo)
    x = x + _L0_ffn_ref(_layernorm(x, axis=-1), L0_ffn_wq, L0_ffn_wk, L0_ffn_wv, L0_ffn_wo, L0_ffn_w1, L0_ffn_w2, L0_ffn_w3, L0_ffn_attn_norm_w, L0_ffn_ff_norm_w, L0_ffn_moe_norm_w, L0_ffn_router_w, L0_ffn_ew1, L0_ffn_ew2, L0_ffn_ew3)
    return x

_drawn_inputs = setup_inputs


def setup_inputs(seed=0):
    import zlib

    import numpy as np

    out = dict(_drawn_inputs(seed))
    spreads = {'L0_ffn_attn_norm_w': (1.0, 0.2),
     'L0_ffn_ff_norm_w': (1.0, 0.2),
     'L0_ffn_moe_norm_w': (1.0, 0.556)}
    factors = {'L0_xattn_bk': 8.0, 'L0_ffn_wq': 6.594, 'L0_ffn_wk': 6.408}
    for name, (base, spread) in spreads.items():
        noise = np.random.default_rng([zlib.crc32(name.encode()), seed]).standard_normal(out[name].shape)
        drawn = base * np.exp(spread * noise) if base else spread * noise
        out[name] = jnp.asarray(drawn.astype(out[name].dtype))
    for name, factor in factors.items():
        out[name] = (out[name] * factor).astype(out[name].dtype)
    return out
```

```python
from contextlib import ExitStack

import concourse.bass as bass
from concourse import mybir

F32 = mybir.dt.float32
F32R = mybir.dt.float32r
BF16 = mybir.dt.bfloat16
ALU = mybir.AluOpType
ACT = mybir.ActivationFunctionType
AX_X = mybir.AxisListType.X

P = 128
D = 128
H = 16
DK = D // H
FF = 512
NE = 8
EH = 128
EPS = 1e-5
SCALE = 1.0 / float(DK) ** 0.5
MASKED = -1e30
TERMS = 3
SROWS = TERMS * TERMS * DK
LAG_EXP, LAG_PV, LAG_POST = 2, 3, 4


def build(nc, x, ctxT, wqT, bq, wkT, bk, wvT, bv, woT, bo, fwq, fwk, fwv, fwo, w1, w2, w3, attn_w, ff_w,
          moe_w, router, ew1, ew2, ew3, out):
    B = x.shape[0]
    NI = 2 * B
    NP = B // 2
    NC = B // 4
    NJ = FF // P + NE
    ND = FF // P

    with ExitStack() as ctx:
        def sb(name, shape, dt=F32):
            return ctx.enter_context(nc.sbuf_tensor(name, shape, dt))

        def pb(name, shape, dt=F32):
            return ctx.enter_context(nc.psum_tensor(name, shape, dt))

        def sem(name):
            return ctx.enter_context(nc.semaphore(name))

        x_sb = sb("x_sb", [P, B, D])
        xn = sb("xn", [P, B, D])
        x2 = sb("x2", [P, B, D])
        xn2 = sb("xn2", [P, B, D])
        hh = xn
        xh = sb("xh", [P, B, D])
        ctxT_sb = sb("ctxT_sb", [P, B * P])
        xnT = sb("xnT", [P, 2, 2 * P])
        xn2T = sb("xn2T", [P, B * P])
        xn2T_hi = sb("xn2T_hi", [P, B * P], F32R)
        xn2T_lo = sb("xn2T_lo", [P, B * P], F32R)
        hT = ctxT_sb[:, 0:4 * P].rearrange("p (a n) -> p a n", a=2)
        hT_hi = sb("hT_hi", [P, B * P], F32R)
        hT_lo = sb("hT_lo", [P, B * P], F32R)
        qk = sb("qk", [P, 2, 2, 2 * P])
        resid = sb("resid", [P, 2, 2 * P])
        parts = sb("parts", [P, 2, 2, TERMS, 2 * P], BF16)
        q_stack = sb("q_stack", [P, NP, H, 2 * P], BF16)
        k_stack = sb("k_stack", [P, NP, H, 2 * P], BF16)
        v_aug = sb("v_aug", [P, B, H, DK + 1])
        negmax = sb("negmax", [P, 2, H])
        maxrow = sb("maxrow", [H, 2, 2, P], BF16)
        probs = sb("probs", [P, 2, H * P])
        o_sb = sb("o_sb", [P, 2, 4 * P])
        rsum = sb("rsum", [P, 2, H])
        o_norm = sb("o_norm", [P, 2, D])
        o_normT = sb("o_normT", [P, 2, P])
        aw = sb("aw", [P, 2, D])
        awn = sb("awn", [P, 2, D])
        junk = sb("junk", [P, D])
        stats = sb("stats", [P, 2, B, 6])
        mv = sb("mv", [P, 2, B, 2])
        ve = sb("ve", [P, 2, B])
        rstd = sb("rstd", [P, 2, B])
        ss = sb("ss", [P, 3, B])
        ms = sb("ms", [P, 3, B])
        rr = sb("rr", [P, 3, B])
        half_neg = sb("half_neg", [P, B])
        ones_row = sb("ones_row", [2, 2 * P], BF16)
        ident = sb("ident", [P, P])
        ident_bf = sb("ident_bf", [P, P], BF16)
        causal_bf = sb("causal_bf", [P, P], BF16)
        wts = {n: sb("w_" + n, [P, D]) for n in ("wqT", "wkT", "wvT", "woT", "fwq", "fwk", "fwv", "fwo")}
        rows = {n: sb("r_" + n, [P, D]) for n in ("bv", "bo", "attn_w", "ff_w", "moe_w")}
        bq_sb = sb("bq_sb", [P, 1])
        bk_sb = sb("bk_sb", [P, 1])
        router_sb = sb("router_sb", [P, NE])
        gate_w = sb("gate_w", [P, NJ * P])
        up_w = sb("up_w", [P, NJ * P])
        gate_hi = sb("gate_hi", [P, NJ * P], F32R)
        gate_lo = sb("gate_lo", [P, NJ * P], F32R)
        up_hi = sb("up_hi", [P, NJ * P], F32R)
        up_lo = sb("up_lo", [P, NJ * P], F32R)
        down_w = sb("down_w", [P, NJ, D])
        logits = sb("logits", [P, B, NE])
        rt = sb("rt", [P, 6, 4, NE])
        rmx = sb("rmx", [P, 2, 4])
        cmp = sb("cmp", [P, 2, 4, NE, NE])
        before = sb("before", [P, NE, NE])
        gates = sb("gates", [P, B, NE])
        ff = probs[:, :, :].rearrange("p a n -> p (a n)")
        g_dense = ff[:, 0:ND * 4 * P].rearrange("p (j n) -> p j n", j=ND)
        g_exp = ff[:, ND * 4 * P:(ND + 2) * 4 * P].rearrange("p (j n) -> p j n", j=2)
        sil = ff[:, (ND + 2) * 4 * P:(ND + 4) * 4 * P].rearrange("p (j n) -> p j n", j=2)
        late = q_stack[:, 0, :, :].rearrange("p h n -> p (h n)").bitcast(F32)
        moe, f_sb, y1, y2 = (late[:, n * 4 * D:(n + 1) * 4 * D].rearrange("p (t d) -> p t d", t=4)
                             for n in range(4))
        y_out = x_sb

        s_qk = pb("s_qk", [P, 8 * P])
        s_kq = pb("s_kq", [P, 8 * P])
        o_ps = pb("o_ps", [P, 4 * P])
        oT_ps = pb("oT_ps", [P, 4 * P])
        m_ps = pb("m_ps", [P, 4 * P])
        f_ps = pb("f_ps", [P, 4 * P])
        hu_ps = [s_qk, s_kq]
        e_ps = [o_ps, oT_ps]
        d_ps = m_ps

        scratch = nc.dram_tensor("parts_dram", (2 * NP, 1 + TERMS, P, TERMS, 2 * P), BF16, kind="Internal").ap()

        ld_x = [sem(f"ld_x{p}") for p in range(NP)]
        ld_ctx = sem("ld_ctx")
        ld_proj = {n: sem("ld_" + n) for n in wts}
        ld_bqk = sem("ld_bqk")
        ld_rows = {n: sem("ldr_" + n) for n in rows}
        ld_router = sem("ld_router")
        ld_up = sem("ld_up")
        ld_down = sem("ld_down")
        consts = sem("consts")
        c_zero = sem("c_zero")
        row_set = sem("row_set")
        k_ones = sem("k_ones")
        ones_set = sem("ones_set")
        pool_chain = sem("pool_chain")
        dve_chain = sem("dve_chain")
        ln_stats = sem("ln_stats")
        ln_rstd = sem("ln_rstd")
        ln1_ready = sem("ln1_ready")
        xbo_ready = sem("xbo_ready")
        ln2_stats = sem("ln2_stats")
        ln2_rstd = sem("ln2_rstd")
        ln2_ready = sem("ln2_ready")
        xnT_ps = sem("xnT_ps")
        xnT_sb = sem("xnT_sb")
        qk_ps = sem("qk_ps")
        qk_sb = sem("qk_sb")
        parts_ready = sem("parts_ready")
        parts_out = sem("parts_out")
        stack = [sem(f"stack{f}") for f in range(2 * NP)]
        v_ps = sem("v_ps")
        v_ready = sem("v_ready")
        xsplit = sem("xsplit")
        sq_ready = sem("sq_ready")
        max_done = sem("max_done")
        maxT_ready = sem("maxT_ready")
        maxrow_ready = sem("maxrow_ready")
        maxrow_in = [sem("maxrow_in0"), sem("maxrow_in1")]
        sk_ready = sem("sk_ready")
        exp_done = sem("exp_done")
        masked = sem("masked")
        pv_done = sem("pv_done")
        o_out = sem("o_out")
        oT_ready = sem("oT_ready")
        rec_done = sem("rec_done")
        on_ready = sem("on_ready")
        onT_ready = sem("onT_ready")
        onT_sb = sem("onT_sb")
        wo_ready = sem("wo_ready")
        wo_read = sem("wo_read")
        x2_done = sem("x2_done")
        st2 = sem("st2")
        ss_a = sem("ss_a")
        rr_a = sem("rr_a")
        awn_done = sem("awn_done")
        h_ready = sem("h_ready")
        hT_psr = sem("hT_psr")
        hT_sb = sem("hT_sb")
        hsplit = sem("hsplit")
        xh_ready = sem("xh_ready")
        wsplit = sem("wsplit")
        rt_shift = sem("rt_shift")
        rt_exp = sem("rt_exp")
        gates_ready = sem("gates_ready")
        up_ready = sem("up_ready")
        silu_done = sem("silu_done")
        g_ready = sem("g_ready")
        down_ready = sem("down_ready")
        acc_step = sem("acc_step")
        dense_ready = sem("dense_ready")
        dense_sb = sem("dense_sb")
        ss_f = sem("ss_f")
        rr_f = sem("rr_f")
        y1_mul = sem("y1_mul")
        y1_ready = sem("y1_ready")
        ss_m = sem("ss_m")
        rr_m = sem("rr_m")
        y2_ready = sem("y2_ready")
        y_ready = sem("y_ready")
        stored = sem("stored")

        def pair_cols(p):
            return slice(2 * P * p, 2 * P * (p + 1))

        def cols(b):
            return slice(P * b, P * (b + 1))

        def in_stack(b):
            return b // 2, slice(P * (b % 2), P * (b % 2 + 1))

        def front_of(slot):
            if slot in (1, 3):
                return 2 + slot // 2
            p, odd = divmod(slot - 2 - LAG_POST, 2)
            return NP + p if not odd and 0 <= p < NP else None

        def hfront_of(slot):
            p, odd = divmod(slot - B - 2 - LAG_POST, 2)
            return p if not odd and 0 <= p < NP else None

        def router_of(slot):
            for c in range(NC):
                if slot == 2 + LAG_POST + 4 * c + 3:
                    return c
            return None

        SLOTS = NI + LAG_POST + 1

        PARTS_OUT = 16 * 2 * TERMS

        block = ctx.enter_context(nc.Block())

        @block.sync
        def _(sp):
            x_v = x.rearrange("b s d -> s b d")
            for p in range(NP):
                sp.dma_start(x_sb[:, 2 * p:2 * p + 2, :], x_v[:, 2 * p:2 * p + 2, :]).then_inc(ld_x[p], 16)
                if p == 0:
                    sp.dma_start(wts["wqT"][:, :], wqT).then_inc(ld_proj["wqT"], 16)
                    sp.dma_start(wts["wkT"][:, :], wkT).then_inc(ld_proj["wkT"], 16)

            def store_parts(f):
                sp.wait_ge(parts_ready, f + 1)
                q, k = parts[:, f % 2, 0], parts[:, f % 2, 1]
                sp.dma_start(scratch[f, 0], q).then_inc(parts_out, 16)
                sp.dma_start(scratch[f, 1], k).then_inc(parts_out, 16)
                for s in range(1, TERMS):
                    sp.dma_start(scratch[f, 1 + s, :, 0:TERMS - s], k[:, s:]).then_inc(parts_out, 16)
                    sp.dma_start(scratch[f, 1 + s, :, TERMS - s:], k[:, :s]).then_inc(parts_out, 16)

            def load_stack(f):
                sp.wait_ge(parts_out, PARTS_OUT * (f + 1))
                if f >= NP:
                    sp.wait_ge(sk_ready, 2 * (2 * (f - NP) + 2))
                p = f % NP
                for s in range(TERMS):
                    r = slice(s * TERMS * DK, (s + 1) * TERMS * DK)
                    for dst, src in ((q_stack, scratch[f, 0]), (k_stack, scratch[f, 1 + s])):
                        sp.dma_start(dst[r, p, :, :], src.rearrange("(h d) t n -> (d t) h n", h=H))\
                            .then_inc(stack[f], 16)

            def maxrows(i):
                sp.wait_ge(maxrow_ready, 2 * (i + 1))
                p, c = in_stack(i % B)
                for t in range(2):
                    sp.dma_start(q_stack[SROWS + t:SROWS + t + 1, p, :, c], maxrow[:, i % 2, t, :])\
                        .then_inc(maxrow_in[i % 2], 16)

            sp.wait_ge(row_set, 1)
            for p in range(NP):
                sp.dma_start(k_stack[SROWS:SROWS + 2, p, :, :],
                             ones_row[:, :].rearrange("r (a n) -> r a n", a=1).broadcast_to([2, H, 2 * P]))\
                    .then_inc(k_ones, 16)
            for f in range(2):
                store_parts(f)
                load_stack(f)
            for n in range(SLOTS):
                if 1 <= n <= NI:
                    maxrows(n - 1)
                f = front_of(n)
                if f is not None:
                    store_parts(f)
                    load_stack(f)
            for c in range(NC):
                for t in range(2):
                    sp.wait_ge(y_ready, 4 * c + 2 * t + 2)
                    b = 4 * c + 2 * t
                    sp.dma_start(out.rearrange("b s d -> s b d")[:, b:b + 2, :], y_out[:, b:b + 2, :])\
                        .then_inc(stored, 16)
            sp.wait_ge(stored, 16 * 2 * NC)

        @block.gpsimd
        def _(pool):
            chain = [0]

            def link(ins):
                chain[0] += 1
                ins.then_inc(pool_chain, 1)
                pool.wait_ge(pool_chain, chain[0])

            pool.memset(ident[:, :], 0.0).then_inc(c_zero, 1)
            pool.memset(half_neg[:, :], -0.5).then_inc(c_zero, 1)
            pool.wait_ge(c_zero, 2)
            pool.affine_select(out=ident[:, :], in_=ident[:, :], compare_op=ALU.not_equal, fill=1.0, base=0,
                               pattern=[[-1, P]], channel_multiplier=1).then_inc(consts, 1)

            def rstd1(p):
                pool.wait_ge(ln_stats, 2 * (p + 1))
                t = slice(2 * p, 2 * p + 2)
                link(pool.tensor_scalar(ve[:, 0, t], mv[:, 0, t, 1], 1.0, EPS, ALU.mult, ALU.add))
                pool.tensor_tensor(rstd[:, 0, t], ve[:, 0, t], half_neg[:, t], ALU.pow).then_inc(ln_rstd, 1)

            rstd1(0)
            rstd1(1)
            link(pool.memset(ident_bf[:, :], 0.0))
            pool.affine_select(out=ident_bf[:, :], in_=ident_bf[:, :], compare_op=ALU.not_equal, fill=1.0,
                               base=0, pattern=[[-1, P]], channel_multiplier=1).then_inc(consts, 1)
            link(pool.memset(causal_bf[:, :], 0.0))
            pool.affine_select(out=causal_bf[:, :], in_=causal_bf[:, :], compare_op=ALU.is_ge, fill=MASKED,
                               base=0, pattern=[[-1, P]], channel_multiplier=1).then_inc(consts, 1)
            link(pool.memset(before[:, :, :], 1.0))
            pool.affine_select(out=before[:, :, :], in_=before[:, :, :], compare_op=ALU.is_gt, fill=0.0,
                               base=0, pattern=[[1, NE], [-1, NE]], channel_multiplier=0).then_inc(consts, 1)
            rstd1(2)
            rstd1(3)

            def split_parts(f):
                pool.wait_ge(qk_sb, f + 1)
                if f >= 2:
                    pool.wait_ge(parts_out, PARTS_OUT * (f - 1))
                s, r, t = qk[:, f % 2], resid[:, :, :], parts[:, f % 2]
                link(pool.tensor_scalar(t[:, :, 0], s, 1.0, 0.0, ALU.mult, ALU.add))
                link(pool.tensor_tensor(r, s, t[:, :, 0], ALU.subtract))
                link(pool.tensor_scalar(t[:, :, 1], r, 1.0, 0.0, ALU.mult, ALU.add))
                pool.tensor_tensor(t[:, :, 2], r, t[:, :, 1], ALU.subtract).then_inc(parts_ready, 1)

            def split_x(f):
                pool.wait_ge(xnT_sb, f + 1)
                c = pair_cols(f - NP)
                link(pool.tensor_scalar(xn2T_hi[:, c], xn2T[:, c], 1.0, 0.0, ALU.mult, ALU.add))
                pool.tensor_tensor(xn2T_lo[:, c], xn2T[:, c], xn2T_hi[:, c].bitcast(F32), ALU.subtract)\
                    .then_inc(xsplit, 1)

            def split_h(p):
                pool.wait_ge(hT_sb, p + 1)
                c = pair_cols(p)
                link(pool.tensor_scalar(hT_hi[:, c], hT[:, p % 2], 1.0, 0.0, ALU.mult, ALU.add))
                pool.tensor_tensor(hT_lo[:, c], hT[:, p % 2], hT_hi[:, c].bitcast(F32), ALU.subtract)\
                    .then_inc(hsplit, 1)

            def split_weights(j):
                c = cols(j)
                for w, hi, lo in ((gate_w, gate_hi, gate_lo), (up_w, up_hi, up_lo)):
                    link(pool.tensor_scalar(hi[:, c], w[:, c], 1.0, 0.0, ALU.mult, ALU.add))
                    pool.tensor_tensor(lo[:, c], w[:, c], hi[:, c].bitcast(F32), ALU.subtract)\
                        .then_inc(wsplit, 1)

            def rstd2(b):
                pool.wait_ge(ln2_stats, b + 1)
                link(pool.tensor_scalar(ve[:, 1, b:b + 1], mv[:, 1, b, 1:2], 1.0, EPS, ALU.mult, ALU.add))
                pool.tensor_tensor(rstd[:, 1, b:b + 1], ve[:, 1, b:b + 1], half_neg[:, b:b + 1], ALU.pow)\
                    .then_inc(ln2_rstd, 1)

            def rms(kind, t):
                link(pool.tensor_scalar(ms[:, kind, t], ss[:, kind, t], 1.0 / D, EPS, ALU.mult, ALU.add))
                return pool.tensor_tensor(rr[:, kind, t], ms[:, kind, t], half_neg[:, t], ALU.pow)

            def mask(i, half):
                pool.wait_ge(exp_done, 2 * i + half + 1)
                v = probs[:, i % 2, 8 * P * half:8 * P * (half + 1)].rearrange("p (h q) -> p h q", h=8)
                pool.affine_select(out=v, in_=v, compare_op=ALU.is_ge, fill=0.0, base=0,
                                   pattern=[[0, 8], [1, P]], channel_multiplier=-1).then_inc(masked, 1)

            pool.wait_ge(ld_rows["bo"], 16)
            for p in range(NP):
                pool.wait_ge(ln1_ready, 2 * p + 2)
                for b in (2 * p, 2 * p + 1):
                    pool.tensor_tensor(x_sb[:, b, :], x_sb[:, b, :], rows["bo"][:, :], ALU.add)\
                        .then_inc(xbo_ready, 1)
            weights_left = list(range(NJ))
            pool.wait_ge(ld_up, 64)
            for n in range(SLOTS):
                f = front_of(n)
                if f is not None:
                    split_parts(f)
                    if f >= NP:
                        split_x(f)
                i = n - LAG_EXP
                if B <= i < NI:
                    mask(i, 0)
                    mask(i, 1)
                if f is None and weights_left:
                    split_weights(weights_left.pop(0))
                    if weights_left:
                        split_weights(weights_left.pop(0))
                b = n - LAG_POST
                if 0 <= b < B:
                    rstd2(b)
                if B <= b < NI:
                    pool.wait_ge(ss_a, b - B + 1)
                    rms(0, slice(b - B, b - B + 1)).then_inc(rr_a, 1)
                b = n - LAG_POST - 1 - B
                if 0 <= b < B:
                    pool.wait_ge(h_ready, b + 1)
                    pool.tensor_tensor(xh[:, b, :], x2[:, b, :], hh[:, b, :], ALU.add).then_inc(xh_ready, 1)
                p = hfront_of(n)
                if p is not None:
                    split_h(p)
            for c in range(NC):
                pool.wait_ge(ss_f, 4 * (c + 1))
                rms(1, slice(4 * c, 4 * c + 4)).then_inc(rr_f, 1)
                for t in range(4):
                    pool.wait_ge(y1_mul, 4 * c + t + 1)
                    pool.tensor_tensor(y1[:, t, :], y1[:, t, :], xh[:, 4 * c + t, :], ALU.add)\
                        .then_inc(y1_ready, 1)
                pool.wait_ge(ss_m, 4 * (c + 1))
                rms(2, slice(4 * c, 4 * c + 4)).then_inc(rr_m, 1)

        @block.scalar
        def _(act):
            act.dma_start(ctxT_sb[:, :], ctxT).then_inc(ld_ctx, 16)
            act.dma_start(bq_sb[:, :], bq.rearrange("(p a) -> p a", a=1)).then_inc(ld_bqk, 16)
            act.dma_start(bk_sb[:, :], bk.rearrange("(p a) -> p a", a=1)).then_inc(ld_bqk, 16)
            act.dma_start(wts["wvT"][:, :], wvT).then_inc(ld_proj["wvT"], 16)

            def row(name, src):
                act.dma_start(rows[name][:, :], bass.AP(tensor=src.tensor, offset=src.offset, ap=[[0, P], [1, D]]))\
                    .then_inc(ld_rows[name], 16)

            row("bv", bv)
            row("bo", bo)
            act.dma_start(wts["woT"][:, :], woT).then_inc(ld_proj["woT"], 16)
            act.dma_start(gate_w[:, 0:FF], w1).then_inc(ld_up, 16)
            act.dma_start(up_w[:, 0:FF], w3).then_inc(ld_up, 16)
            act.dma_start(gate_w[:, FF:].rearrange("p (e h) -> p e h", e=NE), ew1.rearrange("e d h -> d e h"))\
                .then_inc(ld_up, 16)
            act.dma_start(up_w[:, FF:].rearrange("p (e h) -> p e h", e=NE), ew3.rearrange("e d h -> d e h"))\
                .then_inc(ld_up, 16)
            for n, src in (("fwq", fwq), ("fwk", fwk), ("fwv", fwv), ("fwo", fwo)):
                act.dma_start(wts[n][:, :], src).then_inc(ld_proj[n], 16)
            act.dma_start(router_sb[:, :], router).then_inc(ld_router, 16)
            row("attn_w", attn_w)
            act.dma_start(down_w[:, 0:ND, :], w2.rearrange("(j p) d -> p j d", p=P)).then_inc(ld_down, 16)
            act.dma_start(down_w[:, ND:, :], ew2.rearrange("e h d -> h e d")).then_inc(ld_down, 16)
            row("ff_w", ff_w)
            row("moe_w", moe_w)

            def evac_xnT(f):
                act.wait_ge(xnT_ps, f + 1)
                if f < NP:
                    if f >= 2:
                        act.wait_ge(qk_ps, f - 1)
                    dst = xnT[:, f % 2, :]
                else:
                    dst = xn2T[:, pair_cols(f - NP)]
                act.copy(dst, f_ps[:, 0:2 * P]).then_inc(xnT_sb, 1)

            def evac_qk(f):
                act.wait_ge(qk_ps, f + 1)
                if f >= 2:
                    act.wait_ge(parts_ready, f - 1)
                if f < NP:
                    act.wait_ge(ld_bqk, 32)
                    act.activation(qk[:, f % 2, 0], f_ps[:, 0:2 * P], ACT.Identity, bias=bq_sb[:, 0:1])
                    act.activation(qk[:, f % 2, 1], f_ps[:, 2 * P:], ACT.Identity, bias=bk_sb[:, 0:1])\
                        .then_inc(qk_sb, 1)
                else:
                    act.copy(qk[:, f % 2].rearrange("p o n -> p (o n)"), f_ps[:, :]).then_inc(qk_sb, 1)

            def exps(i, half):
                act.wait_ge(sk_ready, 2 * i + half + 1)
                if i >= 2:
                    act.wait_ge(pv_done, 2 * (i - 1))
                act.activation(probs[:, i % 2, 8 * P * half:8 * P * (half + 1)], s_kq[:, :], ACT.Exp,
                               scale=SCALE).then_inc(exp_done, 1)

            def evac_o(i):
                act.wait_ge(pv_done, 2 * (i + 1))
                if i >= 2:
                    act.wait_ge(oT_ready, i - 1)
                act.copy(o_sb[:, i % 2, :], o_ps[:, :]).then_inc(o_out, 1)

            def evac_onT(i):
                act.wait_ge(onT_ready, i + 1)
                if i >= 2:
                    act.wait_ge(wo_ready, i - 1)
                act.copy(o_normT[:, i % 2, :], m_ps[:, 0:P]).then_inc(onT_sb, 1)

            def attn_out(i):
                b = i - B
                act.wait_ge(wo_ready, i + 1)
                if b >= 2:
                    act.wait_ge(awn_done, b - 1)
                act.copy(aw[:, i % 2, :], m_ps[:, 0:P]).then_inc(wo_read, 1)
                act.wait_ge(wo_read, i + 1)
                act.activation(junk[:, :], aw[:, i % 2, :], ACT.Square, accum_out=ss[:, 0, b:b + 1])\
                    .then_inc(ss_a, 1)
                act.wait_ge(ss_a, b + 1)

            for f in range(2):
                evac_xnT(f)
                evac_qk(f)
            for n in range(SLOTS):
                f = front_of(n)
                if f is not None:
                    evac_xnT(f)
                i = n - LAG_EXP
                if 0 <= i < NI:
                    exps(i, 0)
                if f is not None:
                    evac_qk(f)
                j = n - LAG_POST
                if 0 <= j < NI:
                    evac_onT(j)
                p = hfront_of(n)
                if p is not None:
                    act.wait_ge(hT_psr, p + 1)
                    if p >= 2:
                        act.wait_ge(hsplit, p - 1)
                    act.copy(hT[:, p % 2, :], f_ps[:, 0:2 * P]).then_inc(hT_sb, 1)
                if 0 <= i < NI:
                    exps(i, 1)
                if B <= j < NI:
                    attn_out(j)
                k = n - LAG_PV
                if 0 <= k < NI:
                    evac_o(k)
                c = router_of(n)
                if c is not None:
                    act.wait_ge(rt_shift, c + 1)
                    act.activation(rt[:, 1].rearrange("p t e -> p (t e)"), rt[:, 0].rearrange("p t e -> p (t e)"),
                                   ACT.Exp).then_inc(rt_exp, 1)

            def silu(J):
                act.wait_ge(up_ready, J + 1)
                if J >= 2:
                    act.wait_ge(g_ready, J - 1)
                act.activation(sil[:, J % 2, :], hu_ps[J % 2][:, 0:4 * P], ACT.Silu).then_inc(silu_done, 1)

            def squares(kind, src, done, c):
                for t in range(4):
                    act.activation(junk[:, :], src[:, t, :], ACT.Square,
                                   accum_out=ss[:, kind, 4 * c + t:4 * c + t + 1]).then_inc(done, 1)
                    act.wait_ge(done, 4 * c + t + 1)

            for c in range(NC):
                for j in range(NJ):
                    silu(NJ * c + j)
                    if j == ND + 1:
                        act.wait_ge(dense_ready, c + 1)
                        if c:
                            act.wait_ge(y1_mul, 4 * c)
                        act.copy(f_sb[:, :, :].rearrange("p t d -> p (t d)"), d_ps[:, :]).then_inc(dense_sb, 1)
                        act.wait_ge(dense_sb, c + 1)
                        squares(1, f_sb, ss_f, c)
                act.wait_ge(acc_step, 4 * NE * (c + 1))
                squares(2, moe, ss_m, c)

        @block.tensor
        def _(pe):
            def need(sems, count):
                for s in sems:
                    pe.wait_ge(s, count)

            def front_in(f):
                if f >= 1:
                    pe.wait_ge(v_ready, f)
                src = xn if f < NP else xn2
                pe.wait_ge(ln1_ready if f < NP else ln2_ready, 2 * (f % NP) + 2)
                for t in range(2):
                    mm = pe.transpose(f_ps[:, cols(t)], src[:, 2 * (f % NP) + t, :], ident[:, :])
                mm.then_inc(xnT_ps, 1)

            def front_qk(f):
                pe.wait_ge(xnT_sb, f + 1)
                if f == 0:
                    need([ld_proj["wqT"], ld_proj["wkT"], ld_ctx], 16)
                if f == NP:
                    need([ld_proj["fwq"], ld_proj["fwk"]], 16)
                if f < NP:
                    wq, wk, src, ksrc = wts["wqT"], wts["wkT"], xnT[:, f % 2, :], ctxT_sb[:, pair_cols(f)]
                else:
                    wq, wk, src = wts["fwq"], wts["fwk"], xn2T[:, pair_cols(f - NP)]
                    ksrc = src
                pe.matmul(f_ps[:, 0:2 * P], wq[:, :], src, start=True, stop=True)
                pe.matmul(f_ps[:, 2 * P:4 * P], wk[:, :], ksrc, start=True, stop=True).then_inc(qk_ps, 1)

            def front_v(f):
                pe.wait_ge(qk_sb, f + 1)
                if f == 0:
                    need([ld_proj["wvT"]], 16)
                if f == NP:
                    need([ld_proj["fwv"], ld_router], 16)
                for t in range(2):
                    b = 2 * (f % NP) + t
                    src, w = (ctxT_sb, wts["wvT"]) if f < NP else (xn2T, wts["fwv"])
                    mm = pe.matmul(f_ps[:, cols(t)], src[:, cols(b)], w[:, :], start=True, stop=True)
                    if f >= NP:
                        mm = pe.matmul(f_ps[:, 2 * P + NE * t:2 * P + NE * (t + 1)], src[:, cols(b)],
                                       router_sb[:, :], start=True, stop=True)
                mm.then_inc(v_ps, 1)

            def scores_for_max(i, half):
                if half == 0 and i % 2 == 0:
                    pe.wait_ge(stack[i // 2], 16 * 2 * TERMS)
                if i == 0 and half == 0:
                    pe.wait_ge(ones_set, 2)
                    pe.wait_ge(k_ones, 16 * NP)
                if 2 * i + half >= 1:
                    pe.wait_ge(max_done, 2 * i + half)
                p, c = in_stack(i % B)
                causal = i >= B
                if causal:
                    for n in range(2):
                        pe.matmul(s_qk[:, 4 * P * n:4 * P * (n + 1)].rearrange("p (h k) -> p h k", h=4),
                                  ident_bf[:, :],
                                  causal_bf[:, :].rearrange("p (a k) -> p a k", a=1).broadcast_to([P, 4, P]),
                                  start=True, stop=False, skip_group_check=True)
                for n in range(8):
                    h = 8 * half + n
                    mm = pe.matmul(s_qk[:, cols(n)], q_stack[0:SROWS, p, h, c], k_stack[0:SROWS, p, h, c],
                                   start=not causal, stop=True, skip_group_check=causal)
                mm.then_inc(sq_ready, 1)

            def max_transpose(i):
                pe.wait_ge(max_done, 2 * i + 2)
                if i >= LAG_POST:
                    pe.wait_ge(wo_read, i - LAG_POST + 1)
                elif i >= 1:
                    pe.wait_ge(maxrow_ready, 2 * i)
                pe.transpose(m_ps[0:H, 0:P], negmax[:, i % 2, :], ident[:, :]).then_inc(maxT_ready, 1)

            def scores_for_exp(i, half):
                if half == 0:
                    pe.wait_ge(maxrow_in[i % 2], 32 * (i // 2 + 1))
                if 2 * i + half >= 1:
                    pe.wait_ge(exp_done, 2 * i + half)
                p, c = in_stack(i % B)
                for n in range(8):
                    h = 8 * half + n
                    mm = pe.matmul(s_kq[:, cols(n)], k_stack[0:SROWS + 2, p, h, c], q_stack[0:SROWS + 2, p, h, c],
                                   start=True, stop=True)
                mm.then_inc(sk_ready, 1)

            def probs_v(i, half):
                b = i % B
                if half == 0:
                    pe.wait_ge(v_ready, i // 2 + 1)
                    if i >= 1:
                        pe.wait_ge(o_out, i)
                if i >= B:
                    pe.wait_ge(masked, 2 * (i - B) + half + 1)
                else:
                    pe.wait_ge(exp_done, 2 * i + half + 1)
                for n in range(8):
                    h = 8 * half + n
                    g, q = h // 4, h % 4
                    mm = pe.matmul(o_ps[32 * q:32 * q + DK + 1, cols(g)], v_aug[:, b, h, :],
                                   probs[:, i % 2, cols(h)], start=True, stop=True)
                mm.then_inc(pv_done, 1)

            def o_transpose(i):
                pe.wait_ge(o_out, i + 1)
                if i >= 1:
                    pe.wait_ge(on_ready, i)
                for g in range(4):
                    mm = pe.transpose(oT_ps[:, cols(g)], o_sb[:, i % 2, cols(g)], ident[:, :])
                mm.then_inc(oT_ready, 1)

            def on_transpose(i):
                pe.wait_ge(on_ready, i + 1)
                if i + LAG_POST - 1 < NI:
                    pe.wait_ge(maxrow_ready, 2 * (i + LAG_POST))
                else:
                    pe.wait_ge(wo_read, i)
                pe.transpose(m_ps[:, 0:P], o_norm[:, i % 2, :], ident[:, :]).then_inc(onT_ready, 1)

            def project_o(i):
                pe.wait_ge(onT_sb, i + 1)
                if i == 0:
                    need([ld_proj["woT"]], 16)
                if i == B:
                    need([ld_proj["fwo"]], 16)
                pe.matmul(m_ps[:, 0:P], o_normT[:, i % 2, :], (wts["woT"] if i < B else wts["fwo"])[:, :],
                          start=True, stop=True).then_inc(wo_ready, 1)

            def h_transpose(p):
                pe.wait_ge(v_ready, 2 * NP)
                if p >= 1:
                    pe.wait_ge(hT_sb, p)
                pe.wait_ge(h_ready, 2 * p + 2)
                for t in range(2):
                    mm = pe.transpose(f_ps[:, cols(t)], hh[:, 2 * p + t, :], ident[:, :])
                mm.then_inc(hT_psr, 1)

            pe.wait_ge(consts, 1)
            for f in range(2):
                front_in(f)
                front_qk(f)
                front_v(f)
            pe.wait_ge(consts, 3)
            for n in range(SLOTS):
                f, i, k, j = front_of(n), n - LAG_EXP, n - LAG_PV, n - LAG_POST
                if n < NI:
                    scores_for_max(n, 0)
                if 1 <= n <= NI:
                    max_transpose(n - 1)
                if 0 <= j < NI:
                    o_transpose(j)
                if f is not None:
                    front_in(f)
                if 0 <= k < NI:
                    probs_v(k, 0)
                if 0 <= i < NI:
                    scores_for_exp(i, 0)
                if f is not None:
                    front_qk(f)
                if 0 <= j < NI:
                    on_transpose(j)
                if hfront_of(n) is not None:
                    h_transpose(hfront_of(n))
                if n < NI:
                    scores_for_max(n, 1)
                if 0 <= j < NI:
                    project_o(j)
                if f is not None:
                    front_v(f)
                if 0 <= k < NI:
                    probs_v(k, 1)
                if 0 <= i < NI:
                    scores_for_exp(i, 1)

            def up(J):
                c, j = divmod(J, NJ)
                if j == 0:
                    pe.wait_ge(hsplit, 2 * (c + 1))
                    pe.wait_ge(xsplit, 2 * (c + 1))
                if J < 2:
                    pe.wait_ge((max_done, exp_done)[J], 2 * NI)
                    pe.wait_ge(wsplit, 2 * NJ)
                else:
                    pe.wait_ge(g_ready, J - 1)
                hi, lo = (hT_hi, hT_lo) if j < ND else (xn2T_hi, xn2T_lo)
                t = slice(4 * P * c, 4 * P * (c + 1))
                for n, (w_hi, w_lo) in enumerate(((gate_hi, gate_lo), (up_hi, up_lo))):
                    o = hu_ps[J % 2][:, 4 * P * n:4 * P * (n + 1)]
                    pe.matmul(o, w_hi[:, cols(j)], hi[:, t], start=True, stop=False)
                    pe.matmul(o, w_hi[:, cols(j)], lo[:, t], start=False, stop=False)
                    mm = pe.matmul(o, w_lo[:, cols(j)], hi[:, t], start=False, stop=True)
                mm.then_inc(up_ready, 1)

            def down_dense(c):
                pe.wait_ge(g_ready, NJ * c + ND)
                if c == 0:
                    pe.wait_ge(ld_down, 32)
                    pe.wait_ge(wo_read, NI)
                else:
                    pe.wait_ge(dense_sb, c)
                for t in range(4):
                    for j in range(ND):
                        mm = pe.matmul(d_ps[:, cols(t)], g_dense[:, j, cols(t)], down_w[:, j, :],
                                       start=(j == 0), stop=(j == ND - 1))
                mm.then_inc(dense_ready, 1)

            def down_expert(c, e):
                k = NE * c + e
                pe.wait_ge(g_ready, NJ * c + ND + e + 1)
                if k < 2:
                    pe.wait_ge((o_out, on_ready)[k], NI)
                else:
                    pe.wait_ge(acc_step, 4 * (k - 1))
                for t in range(4):
                    mm = pe.matmul(e_ps[k % 2][:, cols(t)], g_exp[:, k % 2, cols(t)], down_w[:, ND + e, :],
                                   start=True, stop=True)
                mm.then_inc(down_ready, 1)

            for c in range(NC):
                for j in range(NJ):
                    up(NJ * c + j)
                    if j == ND:
                        down_dense(c)
                    if j > ND:
                        down_expert(c, j - ND - 1)
                down_expert(c, NE - 1)

        @block.vector
        def _(dve):
            chain = [0]

            def link(ins):
                chain[0] += 1
                ins.then_inc(dve_chain, 1)
                dve.wait_ge(dve_chain, chain[0])

            def ln1_stats(p):
                dve.wait_ge(ld_x[p], 16)
                for b in (2 * p, 2 * p + 1):
                    link(dve.bn_stats(stats[:, 0, b, :], x_sb[:, b, :]))
                    dve.bn_aggr(mv[:, 0, b, :], stats[:, 0, b, :]).then_inc(ln_stats, 1)

            def ln1_apply(p):
                dve.wait_ge(ln_rstd, p + 1)
                for b in (2 * p, 2 * p + 1):
                    dve.tensor_scalar(xn[:, b, :], x_sb[:, b, :], mv[:, 0, b, 0:1], rstd[:, 0, b:b + 1],
                                      ALU.subtract, ALU.mult).then_inc(ln1_ready, 1)

            ln1_stats(0)
            ln1_stats(1)
            dve.memset(ones_row[:, :], 1.0).then_inc(row_set, 1)
            dve.memset(v_aug[:, :, :, DK:DK + 1], 1.0).then_inc(ones_set, 1)
            ln1_apply(0)
            ln1_apply(1)
            dve.memset(o_ps[:, :], 0.0).then_inc(ones_set, 1)

            def split_parts(f):
                dve.wait_ge(qk_sb, f + 1)
                s, r, t = qk[:, f % 2], resid[:, :, :], parts[:, f % 2]
                link(dve.tensor_copy(t[:, :, 0], s))
                link(dve.tensor_tensor(r, s, t[:, :, 0], ALU.subtract))
                link(dve.tensor_copy(t[:, :, 1], r))
                dve.tensor_tensor(t[:, :, 2], r, t[:, :, 1], ALU.subtract).then_inc(parts_ready, 1)

            def take_v(f):
                dve.wait_ge(v_ps, f + 1)
                b = 2 * (f % NP)
                src = f_ps[:, 0:2 * P].rearrange("p (b h d) -> p b h d", b=2, h=H)
                dst = v_aug[:, b:b + 2, :, 0:DK]
                if f < NP:
                    if f == 0:
                        dve.wait_ge(ld_rows["bv"], 16)
                    for t in range(2):
                        ins = dve.tensor_tensor(dst[:, t], src[:, t],
                                                rows["bv"][:, :].rearrange("p (h d) -> p h d", h=H), ALU.add)
                    ins.then_inc(v_ready, 1)
                else:
                    dve.tensor_copy(logits[:, b:b + 2, :].rearrange("p b e -> p (b e)"),
                                    f_ps[:, 2 * P:2 * P + 2 * NE])
                    dve.tensor_copy(dst, src).then_inc(v_ready, 1)

            def maxima(i, half):
                dve.wait_ge(sq_ready, 2 * i + half + 1)
                if i >= 2:
                    dve.wait_ge(maxT_ready, i - 1)
                dve.tensor_reduce(negmax[:, i % 2, 8 * half:8 * half + 8],
                                  s_qk[:, :].rearrange("p (h k) -> p h k", h=8), AX_X, ALU.max, negate=True)\
                    .then_inc(max_done, 1)

            def max_parts(i):
                dve.wait_ge(maxT_ready, i + 1)
                if i >= 2:
                    dve.wait_ge(maxrow_in[i % 2], 32 * (i // 2))
                dve.tensor_copy(maxrow[:, i % 2, 0, :], m_ps[0:H, 0:P]).then_inc(maxrow_ready, 1)
                dve.wait_ge(maxrow_ready, 2 * i + 1)
                dve.tensor_tensor(maxrow[:, i % 2, 1, :], m_ps[0:H, 0:P], maxrow[:, i % 2, 0, :],
                                  ALU.subtract).then_inc(maxrow_ready, 1)

            def normalise(i):
                dve.wait_ge(oT_ready, i + 1)
                if i >= 2:
                    dve.wait_ge(onT_ready, i - 1)
                v = oT_ps[:, :].rearrange("p (h d) -> p h d", h=H)
                dve.reciprocal(rsum[:, i % 2, :], v[:, :, DK]).then_inc(rec_done, 1)
                dve.wait_ge(rec_done, i + 1)
                dve.tensor_tensor(o_norm[:, i % 2, :].rearrange("p (h d) -> p h d", h=H), v[:, :, 0:DK],
                                  rsum[:, i % 2, :].rearrange("p (h a) -> p h a", a=1).broadcast_to([P, H, DK]),
                                  ALU.mult).then_inc(on_ready, 1)

            def residual(b):
                dve.wait_ge(wo_ready, b + 1)
                dve.wait_ge(xbo_ready, b + 1)
                dve.tensor_tensor(x2[:, b, :], m_ps[:, 0:P], x_sb[:, b, :], ALU.add).then_inc(wo_read, 1)
                dve.wait_ge(wo_read, b + 1)
                link(dve.bn_stats(stats[:, 1, b, :], x2[:, b, :]))
                dve.bn_aggr(mv[:, 1, b, :], stats[:, 1, b, :]).then_inc(ln2_stats, 1)

            def ln2_apply(b):
                dve.wait_ge(ln2_rstd, b + 1)
                dve.tensor_scalar(xn2[:, b, :], x2[:, b, :], mv[:, 1, b, 0:1], rstd[:, 1, b:b + 1],
                                  ALU.subtract, ALU.mult).then_inc(ln2_ready, 1)

            def attn_norm(b):
                if b == 0:
                    dve.wait_ge(ld_rows["attn_w"], 16)
                dve.wait_ge(rr_a, b + 1)
                dve.scalar_tensor_tensor(out=awn[:, b % 2, :], in0=aw[:, b % 2, :], scalar=rr[:, 0, b:b + 1],
                                         in1=rows["attn_w"][:, :], op0=ALU.mult, op1=ALU.mult)\
                    .then_inc(awn_done, 1)
                dve.wait_ge(awn_done, b + 1)
                dve.tensor_tensor(hh[:, b, :], awn[:, b % 2, :], xn2[:, b, :], ALU.add).then_inc(h_ready, 1)

            def route_shift(c):
                if c:
                    dve.wait_ge(gates_ready, c)
                lg = logits[:, 4 * c:4 * c + 4, :]
                dve.wait_ge(v_ready, NP + 2 * c + 2)
                link(dve.tensor_reduce(rmx[:, 0, :], lg, AX_X, ALU.max))
                dve.tensor_tensor(rt[:, 0], lg, wide(rmx[:, 0, :]), ALU.subtract).then_inc(rt_shift, 1)

            def wide(v):
                return v.rearrange("p (t a) -> p t a", a=1).broadcast_to([P, 4, NE])

            def route_gates(c):
                dve.wait_ge(rt_exp, c + 1)
                dve.wait_ge(consts, 4)
                link(dve.tensor_reduce(rmx[:, 1, :], rt[:, 1], AX_X, ALU.add))
                link(dve.reciprocal(rmx[:, 0, :], rmx[:, 1, :]))
                link(dve.tensor_tensor(rt[:, 2], rt[:, 1], wide(rmx[:, 0, :]), ALU.mult))
                for t in range(4):
                    other = rt[:, 2, t].rearrange("p (a e) -> p a e", a=1).broadcast_to([P, NE, NE])
                    own = rt[:, 2, t].rearrange("p (e a) -> p e a", a=1).broadcast_to([P, NE, NE])
                    dve.tensor_tensor(cmp[:, 0, t], other, own, ALU.is_gt)
                    link(dve.tensor_tensor(cmp[:, 1, t], other, own, ALU.is_equal))
                    link(dve.tensor_tensor(cmp[:, 1, t], cmp[:, 1, t], before[:, :, :], ALU.mult))
                link(dve.tensor_tensor(cmp[:, 0], cmp[:, 0], cmp[:, 1], ALU.add))
                link(dve.tensor_reduce(rt[:, 3], cmp[:, 0], AX_X, ALU.add))
                dve.scalar_tensor_tensor(out=gates[:, 4 * c:4 * c + 4, :].rearrange("p t e -> p (t e)"),
                                         in0=rt[:, 3].rearrange("p t e -> p (t e)"), scalar=1.5,
                                         in1=rt[:, 2].rearrange("p t e -> p (t e)"),
                                         op0=ALU.is_lt, op1=ALU.mult).then_inc(gates_ready, 1)

            for f in range(2):
                split_parts(f)
                take_v(f)
                ln1_stats(2 + f)
            for f in range(2):
                ln1_apply(2 + f)
            for n in range(SLOTS):
                f, i, k, j = front_of(n), n - LAG_EXP, n - LAG_PV, n - LAG_POST
                if n < NI:
                    maxima(n, 0)
                if 1 <= n <= NI:
                    max_parts(n - 1)
                if 0 <= j < NI:
                    normalise(j)
                if 0 <= j - 1 - B < B:
                    attn_norm(j - 1 - B)
                if n < NI:
                    maxima(n, 1)
                if 0 <= j < B:
                    residual(j)
                if f is not None:
                    take_v(f)
                if router_of(n) is not None:
                    route_shift(router_of(n))
                    route_gates(router_of(n))
                if 0 <= j < B:
                    ln2_apply(j)

            def gated(J):
                c, j = divmod(J, NJ)
                dve.wait_ge(silu_done, J + 1)
                if j < ND:
                    if c:
                        dve.wait_ge(dense_ready, c)
                    dst = g_dense[:, j, :]
                else:
                    k = NE * c + j - ND
                    if k >= 2:
                        dve.wait_ge(down_ready, k - 1)
                    dst = g_exp[:, k % 2, :]
                dve.tensor_tensor(dst, sil[:, J % 2, :], hu_ps[J % 2][:, 4 * P:8 * P], ALU.mult)\
                    .then_inc(g_ready, 1)

            def add_expert(c, e):
                k = NE * c + e
                dve.wait_ge(down_ready, k + 1)
                if e == 0 and c:
                    dve.wait_ge(y2_ready, 4 * c)
                for t in range(4):
                    g = gates[:, 4 * c + t, e:e + 1]
                    src = e_ps[k % 2][:, cols(t)]
                    if e == 0:
                        dve.tensor_scalar(moe[:, t, :], src, g, None, ALU.mult).then_inc(acc_step, 1)
                    else:
                        dve.wait_ge(acc_step, 4 * (k - 1) + t + 1)
                        dve.scalar_tensor_tensor(out=moe[:, t, :], in0=src, scalar=g, in1=moe[:, t, :],
                                                 op0=ALU.mult, op1=ALU.add).then_inc(acc_step, 1)

            for c in range(NC):
                for j in range(NJ):
                    gated(NJ * c + j)
                    if j > ND:
                        add_expert(c, j - ND - 1)
                    if j == ND + 4:
                        if c == 0:
                            dve.wait_ge(ld_rows["ff_w"], 16)
                            dve.wait_ge(ld_rows["moe_w"], 16)
                            dve.wait_ge(xh_ready, B)
                        dve.wait_ge(rr_f, c + 1)
                        if c:
                            dve.wait_ge(y_ready, 4 * c)
                        for t in range(4):
                            dve.scalar_tensor_tensor(out=y1[:, t, :], in0=f_sb[:, t, :],
                                                     scalar=rr[:, 1, 4 * c + t:4 * c + t + 1],
                                                     in1=rows["ff_w"][:, :], op0=ALU.mult, op1=ALU.mult)\
                                .then_inc(y1_mul, 1)
                add_expert(c, NE - 1)
                dve.wait_ge(rr_m, c + 1)
                for t in range(4):
                    dve.scalar_tensor_tensor(out=y2[:, t, :], in0=moe[:, t, :],
                                             scalar=rr[:, 2, 4 * c + t:4 * c + t + 1],
                                             in1=rows["moe_w"][:, :], op0=ALU.mult, op1=ALU.mult)\
                        .then_inc(y2_ready, 1)
                for t in range(4):
                    dve.wait_ge(y2_ready, 4 * c + t + 1)
                    dve.wait_ge(y1_ready, 4 * c + t + 1)
                    dve.tensor_tensor(y_out[:, 4 * c + t, :], y1[:, t, :], y2[:, t, :], ALU.add)\
                        .then_inc(y_ready, 1)


_INS = [("x", None), ("ctx_1024", (2, 0, 1)),
        ("L0_xattn_Wq", (1, 0)), ("L0_xattn_bq", None), ("L0_xattn_Wk", (1, 0)), ("L0_xattn_bk", None),
        ("L0_xattn_Wv", (1, 0)), ("L0_xattn_bv", None), ("L0_xattn_Wo", (1, 0)), ("L0_xattn_bo", None),
        ("L0_ffn_wq", None), ("L0_ffn_wk", None), ("L0_ffn_wv", None), ("L0_ffn_wo", None),
        ("L0_ffn_w1", None), ("L0_ffn_w2", None), ("L0_ffn_w3", None), ("L0_ffn_attn_norm_w", None),
        ("L0_ffn_ff_norm_w", None), ("L0_ffn_moe_norm_w", None), ("L0_ffn_router_w", None),
        ("L0_ffn_ew1", None), ("L0_ffn_ew2", None), ("L0_ffn_ew3", None)]


def kernel(**inputs):
    import numpy as _np
    import concourse.bacc as _bacc
    from concourse import mybir as _mybir
    from concourse.bass_utils import run_bass_kernel_spmd as _run

    nc = _bacc.Bacc("TRN2", target_bir_lowering=False, num_devices=1)
    arrays, args = {}, []
    for name, axes in _INS:
        a = _np.asarray(inputs[name])
        if axes is not None:
            a = a.transpose(axes)
        if name == "ctx_1024":
            a = a.reshape(a.shape[0], -1)
        a = _np.ascontiguousarray(a)
        arrays[f"in_{name}"] = a
        args.append(nc.dram_tensor(f"in_{name}", a.shape, _mybir.dt.from_np(a.dtype), kind="ExternalInput").ap())
    shape = arrays["in_x"].shape
    y = nc.dram_tensor("out_0", shape, _mybir.dt.float32, kind="ExternalOutput").ap()
    build(nc, *args, y)
    r = _run(nc, [arrays], core_ids=[0])
    return r.results[0]["out_0"]
```

```python
from contextlib import ExitStack

import concourse.bass as bass
from concourse import mybir

F32 = mybir.dt.float32
F32R = mybir.dt.float32r
BF16 = mybir.dt.bfloat16
ALU = mybir.AluOpType
ACT = mybir.ActivationFunctionType
AX_X = mybir.AxisListType.X

P = 128
D = 128
H = 16
DK = D // H
FF = 512
NE = 8
EH = 128
EPS = 1e-5
SCALE = 1.0 / float(DK) ** 0.5
MASKED = -1e30
TERMS = 3
SROWS = TERMS * TERMS * DK
QH = 4
NQ = H // QH
LAG_EXP, LAG_POST = 2, 4
LAG_PV = 4 * LAG_EXP + 2
GAP = 1


PROJ_A = ("wqT", "wkT", "bq", "bk")
PROJ_B = ("wvT", "woT", "fwq", "fwk", "fwv", "fwo", "router")
ROWS = ("bv", "bo", "attn_w", "ff_w", "moe_w")


def build(nc, x, ctxT, proj_a, proj_b, row_vectors, gate, up_, down, out):
    B = x.shape[0]
    NI = 2 * B
    NP = B // 2
    NC = B // 4
    NJ = FF // P + NE
    ND = FF // P

    with ExitStack() as ctx:
        def sb(name, shape, dt=F32):
            return ctx.enter_context(nc.sbuf_tensor(name, shape, dt))

        def pb(name, shape, dt=F32):
            return ctx.enter_context(nc.psum_tensor(name, shape, dt))

        def sem(name):
            return ctx.enter_context(nc.semaphore(name))

        x_sb = sb("x_sb", [P, B, D])
        xn = sb("xn", [P, B, D])
        x2 = sb("x2", [P, B, D])
        xn2 = sb("xn2", [P, B, D])
        hh = xn
        xh = sb("xh", [P, B, D])
        ctxT_sb = sb("ctxT_sb", [P, B * P])
        inT = sb("inT", [P, 2, 2 * P])
        xn2T_hi = sb("xn2T_hi", [P, B * P], F32R)
        xn2T_lo = sb("xn2T_lo", [P, B * P], F32R)
        hT = ctxT_sb[:, 0:4 * P].rearrange("p (a n) -> p a n", a=2)
        hT_hi = sb("hT_hi", [P, B * P], F32R)
        hT_lo = sb("hT_lo", [P, B * P], F32R)
        qk = sb("qk", [P, 2, 2, 2 * P])
        resid = sb("resid", [P, 2, 2 * P])
        q_parts = sb("q_parts", [P, 2, TERMS, 2 * P], BF16)
        k_parts = sb("k_parts", [P, 2, 2 * TERMS - 1, 2 * P], BF16)
        q_stack = sb("q_stack", [P, NP, H, 2 * P], BF16)
        k_stack = sb("k_stack", [P, NP, H, 2 * P], BF16)
        v_aug = sb("v_aug", [P, B, H, DK + 1])
        negmax = sb("negmax", [P, 2, H])
        neg_parts = sb("neg_parts", [P, 2, 2, H], BF16)
        maxrow = sb("maxrow", [2 * H, 2, P], BF16)
        probs = sb("probs", [P, 2, H * P])
        o_sb = sb("o_sb", [P, 2, 4 * P])
        rsum = sb("rsum", [P, 2, H])
        o_norm = sb("o_norm", [P, 2, D])
        o_normT = sb("o_normT", [P, 2, P])
        aw = sb("aw", [P, 2, D])
        awn = sb("awn", [P, 2, D])
        junk = sb("junk", [P, D])
        stats = sb("stats", [P, 2, B, 6])
        mv = sb("mv", [P, 2, B, 2])
        ve = sb("ve", [P, 2, B])
        rstd = sb("rstd", [P, 2, B])
        ss = sb("ss", [P, 3, B])
        ms = sb("ms", [P, 3, B])
        rr = sb("rr", [P, 3, B])
        half_neg = sb("half_neg", [P, B])
        ones_row = sb("ones_row", [2, 2 * P], BF16)
        ident = sb("ident", [P, P])
        ident_bf = sb("ident_bf", [P, P], BF16)
        causal_bf = sb("causal_bf", [P, P], BF16)
        pa = sb("pa", list(proj_a.shape))
        pb_ = sb("pb_", list(proj_b.shape))
        wts = {"wqT": pa[:, 0:D], "wkT": pa[:, D:2 * D]}
        bq_sb, bk_sb = pa[:, 2 * D:2 * D + 1], pa[:, 2 * D + 1:2 * D + 2]
        for n, name in enumerate(PROJ_B[:-1]):
            wts[name] = pb_[:, n * D:(n + 1) * D]
        router_sb = pb_[:, (len(PROJ_B) - 1) * D:]
        rows_sb = sb("rows_sb", [P, len(ROWS), D])
        rows = {name: rows_sb[:, n, :] for n, name in enumerate(ROWS)}
        gate_w = sb("gate_w", [P, NJ * P])
        up_w = sb("up_w", [P, NJ * P])
        gate_hi = sb("gate_hi", [P, NJ * P], F32R)
        gate_lo = sb("gate_lo", [P, NJ * P], F32R)
        up_hi = sb("up_hi", [P, NJ * P], F32R)
        up_lo = sb("up_lo", [P, NJ * P], F32R)
        down_w = sb("down_w", [P, NJ, D])
        logits = sb("logits", [P, B, NE])
        rt = sb("rt", [P, 6, 4, NE])
        rmx = sb("rmx", [P, 2, 4])
        cmp = sb("cmp", [P, 2, 4, NE, NE])
        before = sb("before", [P, NE, NE])
        gates = sb("gates", [P, B, NE])
        ff = probs[:, :, :].rearrange("p a n -> p (a n)")
        g_dense = ff[:, 0:ND * 4 * P].rearrange("p (j n) -> p j n", j=ND)
        g_exp = ff[:, ND * 4 * P:(ND + 2) * 4 * P].rearrange("p (j n) -> p j n", j=2)
        sil = qk[:, :, :, :].rearrange("p a o n -> p a (o n)")
        late = q_stack[:, 0, :, :].rearrange("p h n -> p (h n)").bitcast(F32)
        moe, f_sb, y1, y2 = (late[:, n * 4 * D:(n + 1) * 4 * D].rearrange("p (t d) -> p t d", t=4)
                             for n in range(4))
        y_out = x_sb

        s_qk = pb("s_qk", [P, 8 * P])
        s_kq = pb("s_kq", [P, 8 * P])
        o_ps = pb("o_ps", [P, 4 * P])
        oT_ps = pb("oT_ps", [P, 4 * P])
        m_ps = pb("m_ps", [P, 4 * P])
        f_ps = pb("f_ps", [P, 4 * P])
        hu_ps = [s_qk, s_kq]
        e_ps = [o_ps, oT_ps]
        d_ps = m_ps

        scratch = nc.dram_tensor("parts_dram", (2 * NP, 1 + TERMS, P, TERMS * 2 * P), BF16, kind="Internal").ap()

        ld_x = [sem("ld_x0"), sem("ld_x1")]
        ld_ctx = [sem("ld_ctx0"), sem("ld_ctx1")]
        ld_pa = sem("ld_pa")
        ld_pb = sem("ld_pb")
        ld_rows = sem("ld_rows")
        ld_up = sem("ld_up")
        ld_down = sem("ld_down")
        consts = sem("consts")
        c_zero = sem("c_zero")
        row_set = sem("row_set")
        k_ones = sem("k_ones")
        ones_set = sem("ones_set")
        pool_chain = sem("pool_chain")
        dve_chain = sem("dve_chain")
        ln_stats = sem("ln_stats")
        ln_rstd = sem("ln_rstd")
        ln1_ready = sem("ln1_ready")
        xbo_ready = sem("xbo_ready")
        ln2_stats = sem("ln2_stats")
        ln2_rstd = sem("ln2_rstd")
        ln2_ready = sem("ln2_ready")
        xnT_ps = sem("xnT_ps")
        xnT_sb = sem("xnT_sb")
        k_ps = sem("k_ps")
        q_ps = sem("q_ps")
        k_sb = sem("k_sb")
        q_sb = sem("q_sb")
        q_split = sem("q_split")
        k_split = sem("k_split")
        k_wrap = sem("k_wrap")
        q_out = sem("q_out")
        k_out = sem("k_out")
        stack = [sem(f"stack{f}") for f in range(2 * NP)]
        v_ps = sem("v_ps")
        v_ready = sem("v_ready")
        xsplit = sem("xsplit")
        sq_ready = sem("sq_ready")
        max_done = sem("max_done")
        neg_split = sem("neg_split")
        maxT_ready = sem("maxT_ready")
        maxrow_ready = sem("maxrow_ready")
        maxrow_in = [sem("maxrow_in0"), sem("maxrow_in1")]
        sk_ready = sem("sk_ready")
        exp_done = sem("exp_done")
        masked = sem("masked")
        pv_done = sem("pv_done")
        o_out = sem("o_out")
        oT_ready = sem("oT_ready")
        rec_done = sem("rec_done")
        on_ready = sem("on_ready")
        onT_ready = sem("onT_ready")
        onT_sb = sem("onT_sb")
        wo_ready = sem("wo_ready")
        wo_read = sem("wo_read")
        x2_done = sem("x2_done")
        st2 = sem("st2")
        ss_a = sem("ss_a")
        rr_a = sem("rr_a")
        awn_done = sem("awn_done")
        h_ready = sem("h_ready")
        hT_psr = sem("hT_psr")
        hT_sb = sem("hT_sb")
        hsplit = sem("hsplit")
        xh_ready = sem("xh_ready")
        wsplit = sem("wsplit")
        rt_shift = sem("rt_shift")
        rt_exp = sem("rt_exp")
        gates_ready = sem("gates_ready")
        up_ready = sem("up_ready")
        silu_done = sem("silu_done")
        g_ready = sem("g_ready")
        down_ready = sem("down_ready")
        acc_step = sem("acc_step")
        dense_ready = sem("dense_ready")
        dense_sb = sem("dense_sb")
        ss_f = sem("ss_f")
        rr_f = sem("rr_f")
        y1_mul = sem("y1_mul")
        y1_ready = sem("y1_ready")
        ss_m = sem("ss_m")
        rr_m = sem("rr_m")
        y2_ready = sem("y2_ready")
        y_ready = sem("y_ready")
        stored = sem("stored")

        def pair_cols(p):
            return slice(2 * P * p, 2 * P * (p + 1))

        def cols(b):
            return slice(P * b, P * (b + 1))

        def in_stack(b):
            return b // 2, slice(P * (b % 2), P * (b % 2 + 1))

        def front_of(slot):
            if slot in (1, 3):
                return 2 + slot // 2
            p, odd = divmod(slot - 2 - LAG_POST, 2)
            return NP + p if not odd and 0 <= p < NP else None

        def hfront_of(slot):
            p, odd = divmod(slot - B - GAP - 2 - LAG_POST, 2)
            return p if not odd and 0 <= p < NP else None

        def router_of(slot):
            for c in range(NC):
                if slot == 2 + LAG_POST + 4 * c + 3:
                    return c
            return None

        SLOTS = NI + GAP + LAG_POST + 1

        def item_at(slot):
            if 0 <= slot < B:
                return slot
            return slot - GAP if B + GAP <= slot < NI + GAP else None

        def quarter_at(unit):
            i = item_at(unit // NQ)
            return None if i is None else (i, unit % NQ)

        def front_k_ps(f):
            return oT_ps[:, 0:2 * P] if f < 2 else f_ps[:, 2 * P:4 * P]

        def front_v_ps(f):
            return m_ps if f < 2 else f_ps

        EARLY = {(NI + GAP + 1, 3): 0, (NI + GAP + 2, 1): 1, (NI + GAP + 2, 3): 2, (NI + GAP + 3, 1): 3}

        def bank(q):
            return slice(4 * P * (q % 2), 4 * P * (q % 2 + 1))


        block = ctx.enter_context(nc.Block())

        @block.sync
        def _(sp):
            x_v = x.rearrange("b s d -> s b d")
            sp.dma_start(x_sb[:, 0:2, :], x_v[:, 0:2, :]).then_inc(ld_x[0], 16)
            sp.dma_start(ctxT_sb[:, 0:4 * P], ctxT[:, 0:4 * P]).then_inc(ld_ctx[0], 16)
            sp.dma_start(x_sb[:, 2:B, :], x_v[:, 2:B, :]).then_inc(ld_x[1], 16)
            sp.dma_start(ctxT_sb[:, 4 * P:], ctxT[:, 4 * P:]).then_inc(ld_ctx[1], 16)

            def store_parts(f):
                q, k = q_parts[:, f % 2], k_parts[:, f % 2]
                rotations = bass.AP(tensor=k.tensor, offset=k.offset,
                                    ap=[list(k.ap[0]), [2 * P, TERMS], [1, TERMS * 2 * P]])
                sp.wait_ge(q_split, f + 1)
                sp.dma_start(scratch[f, 0], q.rearrange("p t n -> p (t n)")).then_inc(q_out, 16)
                sp.wait_ge(k_split, 2 * (f + 1))
                sp.wait_ge(k_wrap, f + 1)
                sp.dma_start(scratch[f, 1:].rearrange("s p m -> p s m"), rotations).then_inc(k_out, 16)

            def load_stack(f):
                p = f % NP
                if f >= NP:
                    sp.wait_ge(sk_ready, NQ * (2 * (f - NP) + 2))
                for stored, dst, src in ((q_out, q_stack, [0] * TERMS), (k_out, k_stack, range(1, 1 + TERMS))):
                    sp.wait_ge(stored, 16 * (f + 1))
                    for s in range(TERMS):
                        r = slice(s * TERMS * DK, (s + 1) * TERMS * DK)
                        sp.dma_start(dst[r, p, :, :],
                                     scratch[f, src[s]].rearrange("(h d) (t n) -> (d t) h n", h=H, t=TERMS))\
                            .then_inc(stack[f], 16)

            def maxrows(i):
                sp.wait_ge(maxrow_ready, i + 1)
                p, c = in_stack(i % B)
                sp.dma_start(q_stack[SROWS:SROWS + 2, p, :, c], maxrow[:, i % 2, :])\
                    .then_inc(maxrow_in[i % 2], 16)

            store_parts(0)
            load_stack(0)
            sp.wait_ge(row_set, 1)
            sp.dma_start(k_stack[SROWS:SROWS + 2, :, :, :].rearrange("r p h n -> r (p h) n"),
                         ones_row[:, :].rearrange("r (a n) -> r a n", a=1).broadcast_to([2, NP * H, 2 * P]))\
                .then_inc(k_ones, 16)
            store_parts(1)
            load_stack(1)
            for n in range(SLOTS):
                if item_at(n - 1) is not None:
                    maxrows(item_at(n - 1))
                if n == 1:
                    sp.dma_start(gate_w[:, :], gate).then_inc(ld_up, 16)
                    sp.dma_start(up_w[:, :], up_).then_inc(ld_up, 16)
                if n == 3:
                    sp.dma_start(down_w[:, :, :].rearrange("p j d -> p (j d)"), down).then_inc(ld_down, 16)
                if front_of(n - 1) is not None:
                    load_stack(front_of(n - 1))
                if front_of(n) is not None:
                    store_parts(front_of(n))
            for c in range(NC):
                for t in range(2):
                    sp.wait_ge(y_ready, 4 * c + 2 * t + 2)
                    b = 4 * c + 2 * t
                    sp.dma_start(out.rearrange("b s d -> s b d")[:, b:b + 2, :], y_out[:, b:b + 2, :])\
                        .then_inc(stored, 16)
            sp.wait_ge(stored, 16 * 2 * NC)

        @block.gpsimd
        def _(pool):
            chain = [0]

            def link(ins):
                chain[0] += 1
                ins.then_inc(pool_chain, 1)
                pool.wait_ge(pool_chain, chain[0])

            pool.memset(ident[:, :], 0.0).then_inc(c_zero, 1)
            pool.memset(half_neg[:, :], -0.5).then_inc(c_zero, 1)
            pool.wait_ge(c_zero, 2)
            pool.affine_select(out=ident[:, :], in_=ident[:, :], compare_op=ALU.not_equal, fill=1.0, base=0,
                               pattern=[[-1, P]], channel_multiplier=1).then_inc(consts, 1)

            def rstd1(p):
                pool.wait_ge(ln_stats, 2 * (p + 1))
                t = slice(2 * p, 2 * p + 2)
                link(pool.tensor_scalar(ve[:, 0, t], mv[:, 0, t, 1], 1.0, EPS, ALU.mult, ALU.add))
                pool.tensor_tensor(rstd[:, 0, t], ve[:, 0, t], half_neg[:, t], ALU.pow).then_inc(ln_rstd, 1)

            def split_k(f):
                pool.wait_ge(k_sb, f + 1)
                if f >= 2:
                    pool.wait_ge(k_out, 16 * (f - 1))
                s, r, t = qk[:, f % 2, 1], resid[:, 1], k_parts[:, f % 2]
                link(pool.tensor_scalar(t[:, 0], s, 1.0, 0.0, ALU.mult, ALU.add))
                link(pool.tensor_tensor(r, s, t[:, 0], ALU.subtract))
                pool.tensor_scalar(t[:, 1], r, 1.0, 0.0, ALU.mult, ALU.add).then_inc(k_split, 1)
                pool.wait_ge(k_split, 2 * f + 1)
                pool.tensor_tensor(t[:, 2], r, t[:, 1], ALU.subtract).then_inc(k_split, 1)

            def split_x(f):
                pool.wait_ge(xnT_sb, f + 1)
                c, src = pair_cols(f - NP), inT[:, f % 2, :]
                link(pool.tensor_scalar(xn2T_hi[:, c], src, 1.0, 0.0, ALU.mult, ALU.add))
                pool.tensor_tensor(xn2T_lo[:, c], src, xn2T_hi[:, c].bitcast(F32), ALU.subtract)\
                    .then_inc(xsplit, 1)

            def split_h(p):
                pool.wait_ge(hT_sb, p + 1)
                c = pair_cols(p)
                link(pool.tensor_scalar(hT_hi[:, c], hT[:, p % 2], 1.0, 0.0, ALU.mult, ALU.add))
                pool.tensor_tensor(hT_lo[:, c], hT[:, p % 2], hT_hi[:, c].bitcast(F32), ALU.subtract)\
                    .then_inc(hsplit, 1)

            def split_weights(j):
                c = cols(j)
                for w, hi, lo in ((gate_w, gate_hi, gate_lo), (up_w, up_hi, up_lo)):
                    link(pool.tensor_scalar(hi[:, c], w[:, c], 1.0, 0.0, ALU.mult, ALU.add))
                    pool.tensor_tensor(lo[:, c], w[:, c], hi[:, c].bitcast(F32), ALU.subtract)\
                        .then_inc(wsplit, 1)

            def rstd2(b):
                pool.wait_ge(ln2_stats, b + 1)
                pool.tensor_tensor(rstd[:, 1, b:b + 1], ve[:, 1, b:b + 1], half_neg[:, b:b + 1], ALU.pow)\
                    .then_inc(ln2_rstd, 1)

            def rms(kind, t):
                link(pool.tensor_scalar(ms[:, kind, t], ss[:, kind, t], 1.0 / D, EPS, ALU.mult, ALU.add))
                return pool.tensor_tensor(rr[:, kind, t], ms[:, kind, t], half_neg[:, t], ALU.pow)

            def mask(i, q):
                pool.wait_ge(exp_done, NQ * i + q + 1)
                v = probs[:, i % 2, QH * P * q:QH * P * (q + 1)].rearrange("p (h q) -> p h q", h=QH)
                pool.affine_select(out=v, in_=v, compare_op=ALU.is_ge, fill=0.0, base=0,
                                   pattern=[[0, QH], [1, P]], channel_multiplier=-1).then_inc(masked, 1)

            rstd1(0)
            split_k(0)
            rstd1(1)
            split_k(1)
            link(pool.memset(ident_bf[:, :], 0.0))
            pool.affine_select(out=ident_bf[:, :], in_=ident_bf[:, :], compare_op=ALU.not_equal, fill=1.0,
                               base=0, pattern=[[-1, P]], channel_multiplier=1).then_inc(consts, 1)
            link(pool.memset(causal_bf[:, :], 0.0))
            pool.affine_select(out=causal_bf[:, :], in_=causal_bf[:, :], compare_op=ALU.is_ge, fill=MASKED,
                               base=0, pattern=[[-1, P]], channel_multiplier=1).then_inc(consts, 1)
            link(pool.memset(before[:, :, :], 1.0))
            pool.affine_select(out=before[:, :, :], in_=before[:, :, :], compare_op=ALU.is_gt, fill=0.0,
                               base=0, pattern=[[1, NE], [-1, NE]], channel_multiplier=0).then_inc(consts, 1)
            rstd1(2)
            rstd1(3)
            pool.wait_ge(ld_rows, 16)
            for p in range(NP):
                pool.wait_ge(ln1_ready, 2 * p + 2)
                for b in (2 * p, 2 * p + 1):
                    pool.tensor_tensor(x_sb[:, b, :], x_sb[:, b, :], rows["bo"][:, :], ALU.add)\
                        .then_inc(xbo_ready, 1)
            weights_left = list(range(NJ))
            for n in range(SLOTS):
                f, i, j = front_of(n), item_at(n - LAG_EXP), item_at(n - LAG_POST)
                late = item_at(n - LAG_POST - 1)
                own_mask = i is not None and i >= B
                if own_mask:
                    for q in range(NQ - 1):
                        mask(i, q)
                if f is not None:
                    split_k(f)
                if own_mask:
                    mask(i, NQ - 1)
                if j is not None and j < B:
                    rstd2(j)
                if j is not None and j >= B:
                    pool.wait_ge(ss_a, j - B + 1)
                    rms(0, slice(j - B, j - B + 1)).then_inc(rr_a, 1)
                if f is not None and f >= NP:
                    split_x(f)
                if n == 2:
                    pool.wait_ge(ld_up, 32)
                if n >= 2 and f is None:
                    for _ in range(3):
                        if weights_left:
                            split_weights(weights_left.pop(0))
                if late is not None and late >= B:
                    b = late - B
                    pool.wait_ge(h_ready, b + 1)
                    pool.tensor_tensor(xh[:, b, :], x2[:, b, :], hh[:, b, :], ALU.add).then_inc(xh_ready, 1)
                p = hfront_of(n)
                if p is not None:
                    split_h(p)
            for c in range(NC):
                pool.wait_ge(ss_f, 4 * (c + 1))
                rms(1, slice(4 * c, 4 * c + 4)).then_inc(rr_f, 1)
                for t in range(4):
                    pool.wait_ge(y1_mul, 4 * c + t + 1)
                    pool.tensor_tensor(y1[:, t, :], y1[:, t, :], xh[:, 4 * c + t, :], ALU.add)\
                        .then_inc(y1_ready, 1)
                for t in range(0, 4, 2):
                    pool.wait_ge(ss_m, 4 * c + t + 2)
                    rms(2, slice(4 * c + t, 4 * c + t + 2)).then_inc(rr_m, 1)

        @block.scalar
        def _(act):
            act.dma_start(pa[:, :], proj_a).then_inc(ld_pa, 16)
            act.dma_start(rows_sb[:, :, :].rearrange("p r d -> p (r d)"),
                          bass.AP(tensor=row_vectors.tensor, offset=row_vectors.offset,
                                  ap=[[0, P], [1, len(ROWS) * D]])).then_inc(ld_rows, 16)
            act.dma_start(pb_[:, :], proj_b).then_inc(ld_pb, 16)

            def evac_xnT(f):
                act.wait_ge(xnT_ps, f + 1)
                if f >= 2:
                    act.wait_ge(v_ps, f - 1)
                if f >= NP + 2:
                    act.wait_ge(xsplit, f - NP - 1)
                act.copy(inT[:, f % 2, :], f_ps[:, 0:2 * P]).then_inc(xnT_sb, 1)

            def evac_k(f):
                act.wait_ge(k_ps if f < 2 else q_ps, f + 1)
                if f >= 2:
                    act.wait_ge(k_split, 2 * (f - 1))
                if f < NP:
                    ins = act.activation(qk[:, f % 2, 1], front_k_ps(f), ACT.Identity, bias=bk_sb[:, 0:1])
                else:
                    ins = act.copy(qk[:, f % 2, 1], front_k_ps(f))
                ins.then_inc(k_sb, 1)

            def evac_q(f):
                act.wait_ge(q_ps, f + 1)
                if f >= 2:
                    act.wait_ge(q_split, f - 1)
                if f < NP:
                    ins = act.activation(qk[:, f % 2, 0], f_ps[:, 0:2 * P], ACT.Identity, bias=bq_sb[:, 0:1])
                else:
                    ins = act.copy(qk[:, f % 2, 0], f_ps[:, 0:2 * P])
                ins.then_inc(q_sb, 1)

            def exps(i, q):
                act.wait_ge(sk_ready, NQ * i + q + 1)
                if i >= 2:
                    act.wait_ge(pv_done, NQ * (i - 1))
                act.activation(probs[:, i % 2, QH * P * q:QH * P * (q + 1)], s_kq[:, bank(q)], ACT.Exp,
                               scale=SCALE).then_inc(exp_done, 1)

            def take_maxrow(i):
                act.wait_ge(maxT_ready, i + 1)
                if i >= 2:
                    act.wait_ge(maxrow_in[i % 2], 16 * (i // 2))
                act.copy(maxrow[:, i % 2, :], m_ps[0:2 * H, 0:P]).then_inc(maxrow_ready, 1)

            def evac_o(i):
                act.wait_ge(pv_done, NQ * (i + 1))
                if i >= 2:
                    act.wait_ge(oT_ready, 2 * (i - 1))
                act.copy(o_sb[:, i % 2, :], o_ps[:, :]).then_inc(o_out, 1)

            def evac_onT(i):
                act.wait_ge(onT_ready, i + 1)
                if i >= 2:
                    act.wait_ge(wo_ready, i - 1)
                act.copy(o_normT[:, i % 2, :], m_ps[:, 0:P]).then_inc(onT_sb, 1)

            def attn_out(i):
                b = i - B
                act.wait_ge(wo_ready, i + 1)
                if b >= 2:
                    act.wait_ge(awn_done, b - 1)
                act.copy(aw[:, i % 2, :], m_ps[:, 0:P]).then_inc(wo_read, 1)
                act.wait_ge(wo_read, i + 1)
                act.activation(junk[:, :], aw[:, i % 2, :], ACT.Square, accum_out=ss[:, 0, b:b + 1])\
                    .then_inc(ss_a, 1)
                act.wait_ge(ss_a, b + 1)

            evac_xnT(0)
            evac_k(0)
            evac_q(0)
            evac_k(1)
            evac_xnT(1)
            evac_q(1)
            def silu(J):
                act.wait_ge(up_ready, J + 1)
                if J >= 2:
                    act.wait_ge(g_ready, J - 1)
                act.activation(sil[:, J % 2, :], hu_ps[J % 2][:, 0:4 * P], ACT.Silu).then_inc(silu_done, 1)

            for n in range(SLOTS):
                f, i, j = front_of(n), item_at(n - LAG_EXP), item_at(n - LAG_POST)
                pv, p = item_at(n - LAG_EXP - 1), hfront_of(n)
                if i is not None:
                    exps(i, 0)
                if item_at(n - 1) is not None:
                    take_maxrow(item_at(n - 1))
                if f is not None:
                    evac_xnT(f)
                if pv is not None:
                    evac_o(pv)
                if i is not None:
                    exps(i, 1)
                if (n, 1) in EARLY:
                    silu(EARLY[n, 1])
                if j is not None:
                    evac_onT(j)
                if f is not None:
                    evac_k(f)
                    evac_q(f)
                if i is not None:
                    exps(i, 2)
                if j is not None and j >= B:
                    attn_out(j)
                if i is not None:
                    exps(i, 3)
                if p is not None:
                    act.wait_ge(hT_psr, p + 1)
                    if p >= 2:
                        act.wait_ge(hsplit, p - 1)
                    act.copy(hT[:, p % 2, :], f_ps[:, 0:2 * P]).then_inc(hT_sb, 1)
                c = router_of(n)
                if c is not None:
                    act.wait_ge(rt_shift, c + 1)
                    act.activation(rt[:, 4 + c].rearrange("p t e -> p (t e)"),
                                   rt[:, 2 + c].rearrange("p t e -> p (t e)"), ACT.Exp).then_inc(rt_exp, 1)
                if (n, 3) in EARLY:
                    silu(EARLY[n, 3])

            def square(kind, src, done, c, t):
                if 4 * c + t:
                    act.wait_ge(done, 4 * c + t)
                act.activation(junk[:, :], src[:, t, :], ACT.Square,
                               accum_out=ss[:, kind, 4 * c + t:4 * c + t + 1]).then_inc(done, 1)

            def moe_squares(c):
                act.wait_ge(ss_f, 4 * (c + 1))
                for t in range(4):
                    act.wait_ge(acc_step, 4 * (NE * (c + 1) - 1) + t + 1)
                    square(2, moe, ss_m, c, t)

            for c in range(NC):
                for j in range(NJ):
                    if NJ * c + j >= len(EARLY):
                        silu(NJ * c + j)
                    if c and j == 1:
                        moe_squares(c - 1)
                    if j == ND + 1:
                        act.wait_ge(dense_ready, c + 1)
                        if c:
                            act.wait_ge(y1_mul, 4 * c)
                        act.copy(f_sb[:, :, :].rearrange("p t d -> p (t d)"), d_ps[:, :]).then_inc(dense_sb, 1)
                        act.wait_ge(dense_sb, c + 1)
                        act.wait_ge(*((ss_m, 4 * c) if c else (ss_a, B)))
                        for t in range(4):
                            square(1, f_sb, ss_f, c, t)
            moe_squares(NC - 1)

        @block.tensor
        def _(pe):
            def need(sems, count):
                for s in sems:
                    pe.wait_ge(s, count)

            def front_in(f):
                if f == 1:
                    pe.wait_ge(q_sb, 1)
                if f >= 2:
                    pe.wait_ge(v_ready, f)
                src = xn if f < NP else xn2
                pe.wait_ge(ln1_ready if f < NP else ln2_ready, 2 * (f % NP) + 2)
                for t in range(2):
                    mm = pe.transpose(f_ps[:, cols(t)], src[:, 2 * (f % NP) + t, :], ident[:, :])
                mm.then_inc(xnT_ps, 1)

            def front_k(f):
                if f == 0:
                    need([ld_pa, ld_ctx[0]], 16)
                if f == 1:
                    pe.wait_ge(k_sb, 1)
                if f == 2:
                    pe.wait_ge(ld_ctx[1], 16)
                if f >= 2:
                    pe.wait_ge(xnT_sb, f + 1)
                w, src = (wts["wkT"], ctxT_sb[:, pair_cols(f)]) if f < NP else (wts["fwk"], inT[:, f % 2, :])
                pe.matmul(front_k_ps(f), w[:, :], src, start=True, stop=True).then_inc(k_ps, 1)

            def front_q(f):
                pe.wait_ge(xnT_sb, f + 1)
                w = wts["wqT"] if f < NP else wts["fwq"]
                pe.matmul(f_ps[:, 0:2 * P], w[:, :], inT[:, f % 2, :], start=True, stop=True).then_inc(q_ps, 1)

            def front_v(f):
                if f == 0:
                    pe.wait_ge(ld_pb, 16)
                if f == 1:
                    pe.wait_ge(v_ready, 1)
                if f >= 2:
                    pe.wait_ge(q_sb, f + 1)
                o = front_v_ps(f)
                for t in range(2):
                    src = ctxT_sb[:, cols(2 * f + t)] if f < NP else inT[:, f % 2, cols(t)]
                    w = wts["wvT"] if f < NP else wts["fwv"]
                    mm = pe.matmul(o[:, cols(t)], src, w[:, :], start=True, stop=True)
                    if f >= NP:
                        mm = pe.matmul(o[:, 2 * P + NE * t:2 * P + NE * (t + 1)], src,
                                       router_sb[:, :], start=True, stop=True)
                mm.then_inc(v_ps, 1)

            def scores_for_max(i, q):
                u = NQ * i + q
                if q == 0 and i % 2 == 0:
                    pe.wait_ge(stack[i // 2], 16 * 2 * TERMS)
                if u >= 2:
                    pe.wait_ge(max_done, u - 1)
                p, c = in_stack(i % B)
                causal = i >= B
                o = s_qk[:, bank(q)].rearrange("p (h k) -> p h k", h=QH)
                if causal:
                    pe.matmul(o, ident_bf[:, :],
                              causal_bf[:, :].rearrange("p (a k) -> p a k", a=1).broadcast_to([P, QH, P]),
                              start=True, stop=False, skip_group_check=True)
                for n in range(QH):
                    h = QH * q + n
                    mm = pe.matmul(o[:, n], q_stack[0:SROWS, p, h, c], k_stack[0:SROWS, p, h, c],
                                   start=not causal, stop=True, skip_group_check=causal)
                mm.then_inc(sq_ready, 1)

            def max_transpose(n, i):
                pe.wait_ge(neg_split, i + 1)
                if i == 0:
                    pe.wait_ge(v_ready, 2)
                if i >= 1:
                    pe.wait_ge(maxrow_ready, i)
                if item_at(n - 1 - LAG_POST) is not None:
                    pe.wait_ge(wo_read, item_at(n - 1 - LAG_POST) + 1)
                pe.matmul(m_ps[0:2 * H, 0:P], neg_parts[:, i % 2].rearrange("p t h -> p (t h)"), ident_bf[:, :],
                          start=True, stop=True).then_inc(maxT_ready, 1)

            def scores_for_exp(i, q):
                u = NQ * i + q
                if u == 0:
                    pe.wait_ge(k_ones, 16)
                if q == 0:
                    pe.wait_ge(maxrow_in[i % 2], 16 * (i // 2 + 1))
                if u >= 2:
                    pe.wait_ge(exp_done, u - 1)
                p, c = in_stack(i % B)
                o = s_kq[:, bank(q)]
                for n in range(QH):
                    h = QH * q + n
                    mm = pe.matmul(o[:, cols(n)], k_stack[0:SROWS + 2, p, h, c], q_stack[0:SROWS + 2, p, h, c],
                                   start=True, stop=True)
                mm.then_inc(sk_ready, 1)

            def probs_v(i, q):
                b, u = i % B, NQ * i + q
                if u == 0:
                    pe.wait_ge(ones_set, 2)
                if q == 0:
                    pe.wait_ge(v_ready, i // 2 + 1)
                if q == 0 and i >= 1:
                    pe.wait_ge(o_out, i)
                if i >= B:
                    pe.wait_ge(masked, u - NQ * B + 1)
                else:
                    pe.wait_ge(exp_done, u + 1)
                for n in range(QH):
                    h = QH * q + n
                    mm = pe.matmul(o_ps[32 * n:32 * n + DK + 1, cols(q)], v_aug[:, b, h, :],
                                   probs[:, i % 2, cols(h)], start=True, stop=True)
                mm.then_inc(pv_done, 1)

            def o_transpose(i, half):
                pe.wait_ge(o_out, i + 1)
                if i == 0:
                    pe.wait_ge(k_sb, 2)
                if i >= 1:
                    pe.wait_ge(on_ready, i)
                for g in (2 * half, 2 * half + 1):
                    mm = pe.transpose(oT_ps[:, cols(g)], o_sb[:, i % 2, cols(g)], ident[:, :])
                mm.then_inc(oT_ready, 1)

            def on_transpose(n, i):
                pe.wait_ge(on_ready, i + 1)
                if item_at(n - 1) is not None:
                    pe.wait_ge(maxrow_ready, item_at(n - 1) + 1)
                if i >= 1:
                    pe.wait_ge(wo_read, i)
                pe.transpose(m_ps[:, 0:P], o_norm[:, i % 2, :], ident[:, :]).then_inc(onT_ready, 1)

            def project_o(i):
                pe.wait_ge(onT_sb, i + 1)
                pe.matmul(m_ps[:, 0:P], o_normT[:, i % 2, :], (wts["woT"] if i < B else wts["fwo"])[:, :],
                          start=True, stop=True).then_inc(wo_ready, 1)

            def h_transpose(p):
                pe.wait_ge(v_ready, 2 * NP)
                if p >= 1:
                    pe.wait_ge(hT_sb, p)
                pe.wait_ge(h_ready, 2 * p + 2)
                for t in range(2):
                    mm = pe.transpose(f_ps[:, cols(t)], hh[:, 2 * p + t, :], ident[:, :])
                mm.then_inc(hT_psr, 1)

            pe.wait_ge(consts, 1)
            front_in(0)
            front_k(0)
            front_q(0)
            front_k(1)
            front_v(0)
            front_in(1)
            front_q(1)
            front_v(1)
            pe.wait_ge(consts, 3)
            def up(J):
                c, j = divmod(J, NJ)
                if j == 0:
                    pe.wait_ge(hsplit, 2 * (c + 1))
                    pe.wait_ge(xsplit, 2 * (c + 1))
                if J < 2:
                    pe.wait_ge((max_done, exp_done)[J], NQ * NI)
                    pe.wait_ge(wsplit, 2 * NJ)
                else:
                    pe.wait_ge(g_ready, J - 1)
                hi, lo = (hT_hi, hT_lo) if j < ND else (xn2T_hi, xn2T_lo)
                t = slice(4 * P * c, 4 * P * (c + 1))
                for n, (w_hi, w_lo) in enumerate(((gate_hi, gate_lo), (up_hi, up_lo))):
                    o = hu_ps[J % 2][:, 4 * P * n:4 * P * (n + 1)]
                    pe.matmul(o, w_hi[:, cols(j)], hi[:, t], start=True, stop=False)
                    pe.matmul(o, w_hi[:, cols(j)], lo[:, t], start=False, stop=False)
                    mm = pe.matmul(o, w_lo[:, cols(j)], hi[:, t], start=False, stop=True)
                mm.then_inc(up_ready, 1)

            def down_dense(c):
                pe.wait_ge(g_ready, NJ * c + ND)
                if c == 0:
                    pe.wait_ge(ld_down, 16)
                    pe.wait_ge(wo_read, NI)
                else:
                    pe.wait_ge(dense_sb, c)
                for t in range(4):
                    for j in range(ND):
                        mm = pe.matmul(d_ps[:, cols(t)], g_dense[:, j, cols(t)], down_w[:, j, :],
                                       start=(j == 0), stop=(j == ND - 1))
                mm.then_inc(dense_ready, 1)

            def down_expert(c, e):
                k = NE * c + e
                pe.wait_ge(g_ready, NJ * c + ND + e + 1)
                if k < 2:
                    pe.wait_ge((o_out, on_ready)[k], NI)
                else:
                    pe.wait_ge(acc_step, 4 * (k - 1))
                for t in range(4):
                    mm = pe.matmul(e_ps[k % 2][:, cols(t)], g_exp[:, k % 2, cols(t)], down_w[:, ND + e, :],
                                   start=True, stop=True)
                mm.then_inc(down_ready, 1)

            for n in range(SLOTS):
                f, j, ot = front_of(n), item_at(n - LAG_POST), item_at(n - LAG_EXP - 1)
                for q in range(NQ):
                    sq, sk, pv = (quarter_at(NQ * n + q - lag) for lag in (0, NQ * LAG_EXP, LAG_PV))
                    if pv is not None and pv[1] != 0:
                        probs_v(*pv)
                    if sq is not None:
                        scores_for_max(*sq)
                    if sk is not None:
                        scores_for_exp(*sk)
                    if pv is not None and pv[1] == 0:
                        probs_v(*pv)
                    if q == 0:
                        if item_at(n - 1) is not None:
                            max_transpose(n, item_at(n - 1))
                        if f is not None:
                            front_in(f)
                    if q == 1:
                        if f is not None:
                            front_k(f)
                            front_q(f)
                        if j is not None:
                            on_transpose(n, j)
                    if q >= 2 and ot is not None:
                        o_transpose(ot, q - 2)
                    if q == 2 and j is not None:
                        project_o(j)
                    if q == 2 and hfront_of(n) is not None:
                        h_transpose(hfront_of(n))
                    if q == 3 and f is not None:
                        front_v(f)
                    if (n, q) in EARLY:
                        up(EARLY[n, q])

            for c in range(NC):
                for j in range(NJ):
                    if NJ * c + j >= len(EARLY):
                        up(NJ * c + j)
                    if j == ND:
                        down_dense(c)
                    if j > ND:
                        down_expert(c, j - ND - 1)
                down_expert(c, NE - 1)

        @block.vector
        def _(dve):
            chain = [0]

            def link(ins):
                chain[0] += 1
                ins.then_inc(dve_chain, 1)
                dve.wait_ge(dve_chain, chain[0])

            def ln1_stats(p):
                dve.wait_ge(ld_x[min(p, 1)], 16)
                for b in (2 * p, 2 * p + 1):
                    link(dve.bn_stats(stats[:, 0, b, :], x_sb[:, b, :]))
                    dve.bn_aggr(mv[:, 0, b, :], stats[:, 0, b, :]).then_inc(ln_stats, 1)

            def ln1_apply(p):
                dve.wait_ge(ln_rstd, p + 1)
                for b in (2 * p, 2 * p + 1):
                    dve.tensor_scalar(xn[:, b, :], x_sb[:, b, :], mv[:, 0, b, 0:1], rstd[:, 0, b:b + 1],
                                      ALU.subtract, ALU.mult).then_inc(ln1_ready, 1)

            def split_q(f):
                dve.wait_ge(q_sb, f + 1)
                if f >= 2:
                    dve.wait_ge(q_out, 16 * (f - 1))
                s, r, t = qk[:, f % 2, 0], resid[:, 0], q_parts[:, f % 2]
                link(dve.tensor_copy(t[:, 0], s))
                link(dve.tensor_tensor(r, s, t[:, 0], ALU.subtract))
                link(dve.tensor_copy(t[:, 1], r))
                dve.tensor_tensor(t[:, 2], r, t[:, 1], ALU.subtract).then_inc(q_split, 1)

            def wrap_k(f):
                dve.wait_ge(k_split, 2 * f + 1)
                if f >= 2:
                    dve.wait_ge(k_out, 16 * (f - 1))
                dve.tensor_copy(k_parts[:, f % 2, TERMS:], k_parts[:, f % 2, 0:TERMS - 1]).then_inc(k_wrap, 1)

            def take_v(f):
                dve.wait_ge(v_ps, f + 1)
                b = 2 * (f % NP)
                src = front_v_ps(f)[:, 0:2 * P].rearrange("p (b h d) -> p b h d", b=2, h=H)
                dst = v_aug[:, b:b + 2, :, 0:DK]
                if f < NP:
                    if f == 0:
                        dve.wait_ge(ld_rows, 16)
                    for t in range(2):
                        ins = dve.tensor_tensor(dst[:, t], src[:, t],
                                                rows["bv"][:, :].rearrange("p (h d) -> p h d", h=H), ALU.add)
                    ins.then_inc(v_ready, 1)
                else:
                    dve.tensor_copy(logits[:, b:b + 2, :].rearrange("p b e -> p (b e)"),
                                    f_ps[:, 2 * P:2 * P + 2 * NE])
                    dve.tensor_copy(dst, src).then_inc(v_ready, 1)

            def maxima(i, q):
                dve.wait_ge(sq_ready, NQ * i + q + 1)
                dve.tensor_reduce(negmax[:, i % 2, QH * q:QH * (q + 1)],
                                  s_qk[:, bank(q)].rearrange("p (h k) -> p h k", h=QH), AX_X, ALU.max,
                                  negate=True).then_inc(max_done, 1)

            def split_max(i):
                dve.wait_ge(max_done, NQ * (i + 1))
                if i >= 2:
                    dve.wait_ge(maxT_ready, i - 1)
                link(dve.tensor_copy(neg_parts[:, i % 2, 0, :], negmax[:, i % 2, :]))
                dve.tensor_tensor(neg_parts[:, i % 2, 1, :], negmax[:, i % 2, :], neg_parts[:, i % 2, 0, :],
                                  ALU.subtract).then_inc(neg_split, 1)

            def normalise(i):
                dve.wait_ge(oT_ready, 2 * (i + 1))
                if i >= 2:
                    dve.wait_ge(onT_ready, i - 1)
                v = oT_ps[:, :].rearrange("p (h d) -> p h d", h=H)
                dve.reciprocal(rsum[:, i % 2, :], v[:, :, DK]).then_inc(rec_done, 1)
                dve.wait_ge(rec_done, i + 1)
                dve.tensor_tensor(o_norm[:, i % 2, :].rearrange("p (h d) -> p h d", h=H), v[:, :, 0:DK],
                                  rsum[:, i % 2, :].rearrange("p (h a) -> p h a", a=1).broadcast_to([P, H, DK]),
                                  ALU.mult).then_inc(on_ready, 1)

            def residual(b):
                dve.wait_ge(wo_ready, b + 1)
                dve.wait_ge(xbo_ready, b + 1)
                dve.tensor_tensor(x2[:, b, :], m_ps[:, 0:P], x_sb[:, b, :], ALU.add).then_inc(wo_read, 1)
                dve.wait_ge(wo_read, b + 1)
                link(dve.bn_stats(stats[:, 1, b, :], x2[:, b, :]))
                link(dve.bn_aggr(mv[:, 1, b, :], stats[:, 1, b, :]))
                dve.tensor_scalar(ve[:, 1, b:b + 1], mv[:, 1, b, 1:2], EPS, None, ALU.add).then_inc(ln2_stats, 1)

            def ln2_apply(b):
                dve.wait_ge(ln2_rstd, b + 1)
                dve.tensor_scalar(xn2[:, b, :], x2[:, b, :], mv[:, 1, b, 0:1], rstd[:, 1, b:b + 1],
                                  ALU.subtract, ALU.mult).then_inc(ln2_ready, 1)

            def attn_norm(b):
                dve.wait_ge(rr_a, b + 1)
                dve.scalar_tensor_tensor(out=awn[:, b % 2, :], in0=aw[:, b % 2, :], scalar=rr[:, 0, b:b + 1],
                                         in1=rows["attn_w"][:, :], op0=ALU.mult, op1=ALU.mult)\
                    .then_inc(awn_done, 1)
                dve.wait_ge(awn_done, b + 1)
                dve.tensor_tensor(hh[:, b, :], awn[:, b % 2, :], xn2[:, b, :], ALU.add).then_inc(h_ready, 1)

            def route_shift(c):
                lg = logits[:, 4 * c:4 * c + 4, :]
                dve.wait_ge(v_ready, NP + 2 * c + 2)
                if c:
                    dve.wait_ge(rt_shift, c)
                link(dve.tensor_reduce(rmx[:, 0, :], lg, AX_X, ALU.max))
                dve.tensor_tensor(rt[:, 2 + c], lg, wide(rmx[:, 0, :]), ALU.subtract).then_inc(rt_shift, 1)

            def wide(v):
                return v.rearrange("p (t a) -> p t a", a=1).broadcast_to([P, 4, NE])

            def route_gates(c):
                dve.wait_ge(rt_exp, c + 1)
                if c:
                    dve.wait_ge(gates_ready, c)
                dve.wait_ge(consts, 4)
                link(dve.tensor_reduce(rmx[:, 1, :], rt[:, 4 + c], AX_X, ALU.add))
                link(dve.reciprocal(rmx[:, 0, :], rmx[:, 1, :]))
                link(dve.tensor_tensor(rt[:, 0], rt[:, 4 + c], wide(rmx[:, 0, :]), ALU.mult))
                for t in range(4):
                    other = rt[:, 0, t].rearrange("p (a e) -> p a e", a=1).broadcast_to([P, NE, NE])
                    own = rt[:, 0, t].rearrange("p (e a) -> p e a", a=1).broadcast_to([P, NE, NE])
                    dve.tensor_tensor(cmp[:, 0, t], other, own, ALU.is_gt)
                    link(dve.tensor_tensor(cmp[:, 1, t], other, own, ALU.is_equal))
                    link(dve.tensor_tensor(cmp[:, 1, t], cmp[:, 1, t], before[:, :, :], ALU.mult))
                link(dve.tensor_tensor(cmp[:, 0], cmp[:, 0], cmp[:, 1], ALU.add))
                link(dve.tensor_reduce(rt[:, 1], cmp[:, 0], AX_X, ALU.add))
                dve.scalar_tensor_tensor(out=gates[:, 4 * c:4 * c + 4, :].rearrange("p t e -> p (t e)"),
                                         in0=rt[:, 1].rearrange("p t e -> p (t e)"), scalar=1.5,
                                         in1=rt[:, 0].rearrange("p t e -> p (t e)"),
                                         op0=ALU.is_lt, op1=ALU.mult).then_inc(gates_ready, 1)

            def gated(J):
                c, j = divmod(J, NJ)
                dve.wait_ge(silu_done, J + 1)
                if j < ND:
                    if c:
                        dve.wait_ge(dense_ready, c)
                    else:
                        dve.wait_ge(pv_done, NQ * (NI - 1))
                    dst = g_dense[:, j, :]
                else:
                    k = NE * c + j - ND
                    if k >= 2:
                        dve.wait_ge(down_ready, k - 1)
                    else:
                        dve.wait_ge(pv_done, NQ * NI)
                    dst = g_exp[:, k % 2, :]
                dve.tensor_tensor(dst, sil[:, J % 2, :], hu_ps[J % 2][:, 4 * P:8 * P], ALU.mult)\
                    .then_inc(g_ready, 1)

            ln1_stats(0)
            dve.memset(ones_row[:, :], 1.0).then_inc(row_set, 1)
            ln1_apply(0)
            dve.memset(v_aug[:, :, :, DK:DK + 1], 1.0).then_inc(ones_set, 1)
            ln1_stats(1)
            split_q(0)
            wrap_k(0)
            ln1_apply(1)
            take_v(0)
            dve.memset(o_ps[:, :], 0.0).then_inc(ones_set, 1)
            split_q(1)
            wrap_k(1)
            take_v(1)
            ln1_stats(2)
            ln1_stats(3)
            ln1_apply(2)
            ln1_apply(3)
            for n in range(SLOTS):
                i, f, j, last = item_at(n), front_of(n), item_at(n - LAG_POST), item_at(n - LAG_POST - 1)
                if j is not None:
                    normalise(j)
                if i is not None:
                    maxima(i, 0)
                if last is not None and last < B and last % 2 == 0:
                    ln2_apply(last)
                if last is not None and last >= B:
                    attn_norm(last - B)
                if i is not None:
                    maxima(i, 1)
                    maxima(i, 2)
                if j is not None and j < B:
                    residual(j)
                if i is not None:
                    maxima(i, 3)
                    split_max(i)
                if j is not None and j < B and j % 2:
                    ln2_apply(j)
                if f is not None:
                    split_q(f)
                    take_v(f)
                    wrap_k(f)
                if router_of(n) is not None:
                    route_shift(router_of(n))
                if n > NI + GAP + 1:
                    for J in (J for (slot, q), J in EARLY.items() if slot == n and q == 1 or slot == n - 1 and q == 3):
                        gated(J)

            def add_expert(c, e):
                k = NE * c + e
                dve.wait_ge(down_ready, k + 1)
                if e == 0:
                    dve.wait_ge(gates_ready, c + 1)
                if e == 0 and c:
                    dve.wait_ge(y2_ready, 4 * c)
                for t in range(4):
                    g = gates[:, 4 * c + t, e:e + 1]
                    src = e_ps[k % 2][:, cols(t)]
                    if e == 0:
                        dve.tensor_scalar(moe[:, t, :], src, g, None, ALU.mult).then_inc(acc_step, 1)
                    else:
                        dve.wait_ge(acc_step, 4 * (k - 1) + t + 1)
                        dve.scalar_tensor_tensor(out=moe[:, t, :], in0=src, scalar=g, in1=moe[:, t, :],
                                                 op0=ALU.mult, op1=ALU.add).then_inc(acc_step, 1)

            def finish(c):
                for t in range(4):
                    dve.wait_ge(rr_m, 2 * c + t // 2 + 1)
                    dve.scalar_tensor_tensor(out=y2[:, t, :], in0=moe[:, t, :],
                                             scalar=rr[:, 2, 4 * c + t:4 * c + t + 1],
                                             in1=rows["moe_w"][:, :], op0=ALU.mult, op1=ALU.mult)\
                        .then_inc(y2_ready, 1)
                    if t % 2:
                        for u in (t - 1, t):
                            dve.wait_ge(y2_ready, 4 * c + u + 1)
                            dve.wait_ge(y1_ready, 4 * c + u + 1)
                            dve.tensor_tensor(y_out[:, 4 * c + u, :], y1[:, u, :], y2[:, u, :], ALU.add)\
                                .then_inc(y_ready, 1)

            for c in range(NC):
                for j in range(NJ):
                    if NJ * c + j >= len(EARLY):
                        gated(NJ * c + j)
                    if c and j == 2:
                        finish(c - 1)
                    if j == ND:
                        route_gates(c)
                    if j > ND:
                        add_expert(c, j - ND - 1)
                    if j == ND + 4:
                        if c == 0:
                            dve.wait_ge(xh_ready, B)
                        dve.wait_ge(rr_f, c + 1)
                        if c:
                            dve.wait_ge(y_ready, 4 * c)
                        for t in range(4):
                            dve.scalar_tensor_tensor(out=y1[:, t, :], in0=f_sb[:, t, :],
                                                     scalar=rr[:, 1, 4 * c + t:4 * c + t + 1],
                                                     in1=rows["ff_w"][:, :], op0=ALU.mult, op1=ALU.mult)\
                                .then_inc(y1_mul, 1)
                add_expert(c, NE - 1)
            finish(NC - 1)


def kernel(**inputs):
    import numpy as _np
    import concourse.bacc as _bacc
    from concourse import mybir as _mybir
    from concourse.bass_utils import run_bass_kernel_spmd as _run

    nc = _bacc.Bacc("TRN2", target_bir_lowering=False, num_devices=1)
    a = {name: _np.asarray(v) for name, v in inputs.items()}
    xa = {n: a["L0_xattn_" + n] for n in ("Wq", "bq", "Wk", "bk", "Wv", "bv", "Wo", "bo")}
    fa = {n[len("L0_ffn_"):]: v for n, v in a.items() if n.startswith("L0_ffn_")}

    def blocks(w):
        return w.reshape(-1, EH, D).transpose(1, 0, 2).reshape(EH, -1)

    def beside(w):
        return w.transpose(1, 0, 2).reshape(D, -1)

    side = lambda *parts: _np.concatenate(parts, axis=1)
    arrays = {
        "in_x": a["x"],
        "in_ctxT": a["ctx_1024"].transpose(2, 0, 1).reshape(D, -1),
        "in_proj_a": side(xa["Wq"].T, xa["Wk"].T, xa["bq"][:, None], xa["bk"][:, None]),
        "in_proj_b": side(xa["Wv"].T, xa["Wo"].T, fa["wq"], fa["wk"], fa["wv"], fa["wo"], fa["router_w"]),
        "in_rows": _np.concatenate([xa["bv"], xa["bo"], fa["attn_norm_w"], fa["ff_norm_w"], fa["moe_norm_w"]]),
        "in_gate": side(fa["w1"], beside(fa["ew1"])),
        "in_up": side(fa["w3"], beside(fa["ew3"])),
        "in_down": side(blocks(fa["w2"]), blocks(fa["ew2"])),
    }
    arrays = {name: _np.ascontiguousarray(v) for name, v in arrays.items()}
    args = [nc.dram_tensor(name, v.shape, _mybir.dt.from_np(v.dtype), kind="ExternalInput").ap()
            for name, v in arrays.items()]
    y = nc.dram_tensor("out_0", a["x"].shape, _mybir.dt.float32, kind="ExternalOutput").ap()
    build(nc, *args, y)
    r = _run(nc, [arrays], core_ids=[0])
    return r.results[0]["out_0"]
```

```python
from contextlib import ExitStack

import concourse.bass as bass
from concourse import mybir

F32 = mybir.dt.float32
F32R = mybir.dt.float32r
BF16 = mybir.dt.bfloat16
ALU = mybir.AluOpType
ACT = mybir.ActivationFunctionType
AX_X = mybir.AxisListType.X

P = 128
D = 128
H = 16
DK = D // H
FF = 512
NE = 8
EH = 128
EPS = 1e-5
SCALE = 1.0 / float(DK) ** 0.5
MASKED = -1e30
TERMS = 3
SROWS = TERMS * TERMS * DK
QH = 4
NQ = H // QH
LAG_POST = 4
GAP = 1

PROJ_A = ("wqT", "wkT", "bq", "bk")
PROJ_B = ("wvT", "woT", "fwq", "fwk", "fwv", "fwo", "router")
ROWS = ("bv", "bo", "attn_w", "ff_w", "moe_w")


def build(nc, x, ctxT, proj_a, proj_b, row_vectors, gate, up_w_in, down, out):
    B = x.shape[0]
    NI = 2 * B
    NP = B // 2
    NC = B // 4
    NJ = FF // P + NE
    ND = FF // P

    with ExitStack() as ctx:
        def sb(name, shape, dt=F32):
            return ctx.enter_context(nc.sbuf_tensor(name, shape, dt))

        def pb(name, shape, dt=F32):
            return ctx.enter_context(nc.psum_tensor(name, shape, dt))

        def sem(name):
            return ctx.enter_context(nc.semaphore(name))

        x_sb = sb("x_sb", [P, B, D])
        xn = sb("xn", [P, B, D])
        x2 = sb("x2", [P, B, D])
        xn2 = sb("xn2", [P, B, D])
        hh = xn
        xh = sb("xh", [P, B, D])
        ctxT_sb = sb("ctxT_sb", [P, B * P])
        inT = sb("inT", [P, 2, 2 * P])
        xn2T_hi = sb("xn2T_hi", [P, B * P], F32R)
        xn2T_lo = sb("xn2T_lo", [P, B * P], F32R)
        hT = ctxT_sb[:, 0:4 * P].rearrange("p (a n) -> p a n", a=2)
        hT_hi = sb("hT_hi", [P, B * P], F32R)
        hT_lo = sb("hT_lo", [P, B * P], F32R)
        qk = sb("qk", [P, 2, 2, 2 * P])
        resid = sb("resid", [P, 2, 2 * P])
        q_parts = sb("q_parts", [P, 2, TERMS, 2 * P], BF16)
        k_parts = sb("k_parts", [P, 2, 2 * TERMS - 1, 2 * P], BF16)
        q_stack = sb("q_stack", [P, NP, H, 2 * P], BF16)
        k_stack = sb("k_stack", [P, NP, H, 2 * P], BF16)
        v_aug = sb("v_aug", [P, B, H, DK + 1])
        negmax = sb("negmax", [P, 2, H])
        neg_parts = sb("neg_parts", [P, 2, 2, H], BF16)
        maxrow = sb("maxrow", [2 * H, 2, P], BF16)
        probs = sb("probs", [P, 2, H * P])
        o_sb = sb("o_sb", [P, 2, 4 * P])
        rsum = sb("rsum", [P, 2, H])
        o_norm = sb("o_norm", [P, 2, D])
        o_normT = sb("o_normT", [P, 2, P])
        aw = sb("aw", [P, 2, D])
        awn = sb("awn", [P, 2, D])
        junk = sb("junk", [P, D])
        stats = sb("stats", [P, 2, B, 6])
        mv = sb("mv", [P, 2, B, 2])
        ve = sb("ve", [P, 2, B])
        rstd = sb("rstd", [P, 2, B])
        ss = sb("ss", [P, 3, B])
        ms = sb("ms", [P, 3, B])
        rr = sb("rr", [P, 3, B])
        half_neg = sb("half_neg", [P, B])
        ones_row = sb("ones_row", [2, 2 * P], BF16)
        ident = sb("ident", [P, P])
        ident_bf = sb("ident_bf", [P, P], BF16)
        causal_bf = sb("causal_bf", [P, P], BF16)
        pa_sb = sb("pa_sb", list(proj_a.shape))
        pb_sb = sb("pb_sb", list(proj_b.shape))
        wts = {"wqT": pa_sb[:, 0:D], "wkT": pa_sb[:, D:2 * D]}
        bq_sb, bk_sb = pa_sb[:, 2 * D:2 * D + 1], pa_sb[:, 2 * D + 1:2 * D + 2]
        for n, name in enumerate(PROJ_B[:-1]):
            wts[name] = pb_sb[:, n * D:(n + 1) * D]
        router_sb = pb_sb[:, (len(PROJ_B) - 1) * D:]
        rows_sb = sb("rows_sb", [P, len(ROWS), D])
        rows = {name: rows_sb[:, n, :] for n, name in enumerate(ROWS)}
        gate_w = sb("gate_w", [P, NJ * P])
        up_w = sb("up_w", [P, NJ * P])
        gate_hi = sb("gate_hi", [P, NJ * P], F32R)
        gate_lo = sb("gate_lo", [P, NJ * P], F32R)
        up_hi = sb("up_hi", [P, NJ * P], F32R)
        up_lo = sb("up_lo", [P, NJ * P], F32R)
        down_w = sb("down_w", [P, NJ, D])
        logits = sb("logits", [P, B, NE])
        rt = sb("rt", [P, 6, 4, NE])
        rmx = sb("rmx", [P, 2, 4])
        cmp = sb("cmp", [P, 2, 4, NE, NE])
        before = sb("before", [P, NE, NE])
        gates = sb("gates", [P, B, NE])
        ff = probs[:, :, :].rearrange("p a n -> p (a n)")
        g_dense = ff[:, 0:ND * 4 * P].rearrange("p (j n) -> p j n", j=ND)
        g_exp = ff[:, ND * 4 * P:(ND + 2) * 4 * P].rearrange("p (j n) -> p j n", j=2)
        sil = qk[:, :, :, :].rearrange("p a o n -> p a (o n)")
        late = q_stack[:, 0, :, :].rearrange("p h n -> p (h n)").bitcast(F32)
        moe, f_sb, y1, y2 = (late[:, n * 4 * D:(n + 1) * 4 * D].rearrange("p (t d) -> p t d", t=4)
                             for n in range(4))
        y_out = x_sb

        s_qk = pb("s_qk", [P, 8 * P])
        s_kq = pb("s_kq", [P, 8 * P])
        o_ps = pb("o_ps", [P, 4 * P])
        oT_ps = pb("oT_ps", [P, 4 * P])
        m_ps = pb("m_ps", [P, 4 * P])
        f_ps = pb("f_ps", [P, 4 * P])
        hu_ps = [s_qk, s_kq]
        e_ps = [oT_ps, m_ps]
        d_ps = o_ps

        scratch = nc.dram_tensor("parts_dram", (2 * NP, 1 + TERMS, P, TERMS * 2 * P), BF16, kind="Internal").ap()

        ld_x = [sem("ld_x0"), sem("ld_x1")]
        ld_ctx = [sem("ld_ctx0"), sem("ld_ctx1")]
        ld_pa = sem("ld_pa")
        ld_pb = sem("ld_pb")
        ld_rows = sem("ld_rows")
        ld_up = sem("ld_up")
        ld_down = sem("ld_down")
        consts = sem("consts")
        c_zero = sem("c_zero")
        row_set = sem("row_set")
        k_ones = sem("k_ones")
        ones_set = sem("ones_set")
        pool_chain = sem("pool_chain")
        dve_chain = sem("dve_chain")
        ln_stats = sem("ln_stats")
        ln_rstd = sem("ln_rstd")
        ln1_ready = sem("ln1_ready")
        xbo_ready = sem("xbo_ready")
        ln2_stats = sem("ln2_stats")
        ln2_rstd = sem("ln2_rstd")
        ln2_ready = sem("ln2_ready")
        xnT_ps = sem("xnT_ps")
        xnT_sb = sem("xnT_sb")
        k_ps = sem("k_ps")
        q_ps = sem("q_ps")
        k_sb = sem("k_sb")
        q_sb = sem("q_sb")
        q_rest = sem("q_rest")
        q_split = sem("q_split")
        k_split = sem("k_split")
        k_wrap = sem("k_wrap")
        q_out = sem("q_out")
        k_out = sem("k_out")
        stack = [sem(f"stack{f}") for f in range(2 * NP)]
        v_ps = sem("v_ps")
        v_ready = sem("v_ready")
        xsplit = sem("xsplit")
        sq_ready = sem("sq_ready")
        max_done = sem("max_done")
        neg_hi = sem("neg_hi")
        neg_split = sem("neg_split")
        maxT_ready = sem("maxT_ready")
        maxrow_ready = sem("maxrow_ready")
        maxrow_in = [sem("maxrow_in0"), sem("maxrow_in1")]
        sk_ready = sem("sk_ready")
        exp_done = sem("exp_done")
        masked = sem("masked")
        pv_done = sem("pv_done")
        o_out = sem("o_out")
        oT_ready = sem("oT_ready")
        rec_done = sem("rec_done")
        on_ready = sem("on_ready")
        onT_ready = sem("onT_ready")
        onT_sb = sem("onT_sb")
        wo_ready = sem("wo_ready")
        wo_read = sem("wo_read")
        st2 = sem("st2")
        ss_a = sem("ss_a")
        rr_a = sem("rr_a")
        awn_done = sem("awn_done")
        h_ready = sem("h_ready")
        hT_psr = sem("hT_psr")
        hT_sb = sem("hT_sb")
        hsplit = sem("hsplit")
        xh_ready = sem("xh_ready")
        wsplit = sem("wsplit")
        rt_shift = sem("rt_shift")
        rt_exp = sem("rt_exp")
        gates_ready = sem("gates_ready")
        up_ready = sem("up_ready")
        silu_done = sem("silu_done")
        g_ready = sem("g_ready")
        down_ready = sem("down_ready")
        acc_step = sem("acc_step")
        dense_ready = sem("dense_ready")
        dense_sb = sem("dense_sb")
        ss_f = sem("ss_f")
        rr_f = sem("rr_f")
        y1_mul = sem("y1_mul")
        y1_ready = sem("y1_ready")
        ss_m = sem("ss_m")
        rr_m = sem("rr_m")
        y2_ready = sem("y2_ready")
        y_ready = sem("y_ready")
        stored = sem("stored")

        def pair_cols(p):
            return slice(2 * P * p, 2 * P * (p + 1))

        def cols(b):
            return slice(P * b, P * (b + 1))

        def in_stack(b):
            return b // 2, slice(P * (b % 2), P * (b % 2 + 1))

        LATE_CROSS_FRONTS = (1, 3)

        def front_of(slot):
            if slot in LATE_CROSS_FRONTS:
                return 2 + LATE_CROSS_FRONTS.index(slot)
            p, odd = divmod(slot - 2 - LAG_POST, 2)
            return NP + p if not odd and 0 <= p < NP else None

        def hfront_of(slot):
            p, odd = divmod(slot - B - GAP - 2 - LAG_POST, 2)
            return p if not odd and 0 <= p < NP else None

        def router_of(slot):
            for c in range(NC):
                if slot == 2 + LAG_POST + 4 * c + 3:
                    return c
            return None

        SLOTS = NI + GAP + LAG_POST + 2

        def item_at(slot):
            if 0 <= slot < B:
                return slot
            return slot - GAP if B + GAP <= slot < NI + GAP else None

        def cross_at(slot, odd=None):
            i = item_at(slot)
            return i if i is not None and i < B and odd in (None, i % 2) else None

        def self_at(slot):
            i = item_at(slot)
            return i if i is not None and i >= B else None

        def self_front_of(slot):
            f = front_of(slot)
            return f if f is not None and f >= NP else None

        def cross_front_of(slot):
            f = front_of(slot)
            return f if f is not None and f < NP else None

        def at(stage, which, *args):
            if which is not None:
                stage(which, *args)

        def early(table, slot, place):
            return table.get((slot - NI - GAP, place))

        PE_EARLY = {(1, 2): 0, (2, 0): 1, (2, 2): 2, (3, 1): 3, (3, 2): 4}
        ACT_EARLY = {(1, 1): 0, (2, 0): 1, (2, 1): 2, (3, 0): 3, (3, 1): 4}
        DVE_EARLY = {(2, 0): 0, (2, 1): 1, (3, 0): 2, (3, 1): 3, (4, 0): 4}
        WEIGHTS = {(2, 0): 0, (2, 2): 1, (3, 0): 2, (3, 2): 3, (4, 0): 4, (5, 2): 5, (6, 0): 6, (6, 2): 7,
                   (7, 1): 8, (7, 2): 9, (8, 2): 10, (9, 0): 11}

        def front_k_ps(f):
            return oT_ps[:, 0:2 * P] if f < 2 else f_ps[:, 2 * P:4 * P]

        LAST = NE * NC - 1

        def e_out(k, t):
            return (f_ps if k == LAST and t >= 2 else e_ps[k % 2])[:, cols(t)]

        def front_v_ps(f):
            return m_ps if f < NP else f_ps

        def bank(q):
            return slice(4 * P * (q % 2), 4 * P * (q % 2 + 1))

        block = ctx.enter_context(nc.Block())

        @block.sync
        def _(sp):
            x_v = x.rearrange("b s d -> s b d")
            sp.dma_start(x_sb[:, 0:2, :], x_v[:, 0:2, :]).then_inc(ld_x[0], 16)
            sp.dma_start(ctxT_sb[:, 0:4 * P], ctxT[:, 0:4 * P]).then_inc(ld_ctx[0], 16)
            sp.dma_start(x_sb[:, 2:B, :], x_v[:, 2:B, :]).then_inc(ld_x[1], 16)
            sp.dma_start(ctxT_sb[:, 4 * P:], ctxT[:, 4 * P:]).then_inc(ld_ctx[1], 16)

            def store_q(f):
                sp.wait_ge(q_split, f + 1)
                sp.dma_start(scratch[f, 0], q_parts[:, f % 2].rearrange("p t n -> p (t n)")).then_inc(q_out, 16)

            def store_k(f):
                k = k_parts[:, f % 2]
                rotations = bass.AP(tensor=k.tensor, offset=k.offset,
                                    ap=[list(k.ap[0]), [2 * P, TERMS], [1, TERMS * 2 * P]])
                sp.wait_ge(k_split, 2 * (f + 1))
                sp.wait_ge(k_wrap, f + 1)
                sp.dma_start(scratch[f, 1:].rearrange("s p m -> p s m"), rotations).then_inc(k_out, 16)

            def load_rows(f, s, dst, src):
                r = slice(s * TERMS * DK, (s + 1) * TERMS * DK)
                sp.dma_start(dst[r, f % NP, :, :], src.rearrange("(h d) (t n) -> (d t) h n", h=H, t=TERMS))\
                    .then_inc(stack[f], 16)

            def load_q(f):
                if f >= NP:
                    sp.wait_ge(sk_ready, NQ * (2 * (f - NP) + 2))
                sp.wait_ge(q_out, 16 * (f + 1))
                for s in range(TERMS):
                    load_rows(f, s, q_stack, scratch[f, 0])

            def load_k(f):
                if f >= NP:
                    sp.wait_ge(sk_ready, NQ * (2 * (f - NP) + 2))
                sp.wait_ge(k_out, 16 * (f + 1))
                for s in range(TERMS):
                    load_rows(f, s, k_stack, scratch[f, 1 + s])

            def load_weights(n):
                dst, src, done = ((gate_w[:, :], gate, ld_up), (up_w[:, :], up_w_in, ld_up),
                                  (down_w[:, :, :].rearrange("p j d -> p (j d)"), down, ld_down))[n]
                sp.dma_start(dst, src).then_inc(done, 16)

            def set_ones():
                sp.wait_ge(row_set, 1)
                sp.dma_start(k_stack[SROWS:SROWS + 2, :, :, :].rearrange("r p h n -> r (p h) n"),
                             ones_row[:, :].rearrange("r (a n) -> r a n", a=1).broadcast_to([2, NP * H, 2 * P]))\
                    .then_inc(k_ones, 16)

            def maxrows(i):
                sp.wait_ge(maxrow_ready, i + 1)
                p, c = in_stack(i % B)
                sp.dma_start(q_stack[SROWS:SROWS + 2, p, :, c], maxrow[:, i % 2, :])\
                    .then_inc(maxrow_in[i % 2], 16)

            store_q(0)
            store_k(0)
            load_q(0)
            load_k(0)
            set_ones()
            store_q(1)
            store_k(1)
            load_q(1)
            load_k(1)
            for n in range(SLOTS):
                at(load_k, front_of(n - 2))
                at(maxrows, item_at(n - 1))
                at(load_weights, {1: 0}.get(n))
                at(store_q, front_of(n - 1))
                at(store_k, front_of(n - 1))
                at(load_q, front_of(n - 1))
                at(load_weights, {3: 2}.get(n))
                at(load_weights, {1: 1}.get(n))
            for c in range(NC):
                for t in range(2):
                    sp.wait_ge(y_ready, 4 * c + 2 * t + 2)
                    b = 4 * c + 2 * t
                    sp.dma_start(out.rearrange("b s d -> s b d")[:, b:b + 2, :], y_out[:, b:b + 2, :])\
                        .then_inc(stored, 16)
            sp.wait_ge(stored, 16 * 2 * NC)

        @block.gpsimd
        def _(pool):
            chain = [0]

            def link(ins):
                chain[0] += 1
                ins.then_inc(pool_chain, 1)
                pool.wait_ge(pool_chain, chain[0])

            pool.memset(ident[:, :], 0.0).then_inc(c_zero, 1)
            pool.memset(half_neg[:, :], -0.5).then_inc(c_zero, 1)
            pool.wait_ge(c_zero, 2)
            pool.affine_select(out=ident[:, :], in_=ident[:, :], compare_op=ALU.not_equal, fill=1.0, base=0,
                               pattern=[[-1, P]], channel_multiplier=1).then_inc(consts, 1)

            def rstd1(p):
                pool.wait_ge(ln_stats, 2 * (p + 1))
                t = slice(2 * p, 2 * p + 2)
                link(pool.tensor_scalar(ve[:, 0, t], mv[:, 0, t, 1], 1.0, EPS, ALU.mult, ALU.add))
                pool.tensor_tensor(rstd[:, 0, t], ve[:, 0, t], half_neg[:, t], ALU.pow).then_inc(ln_rstd, 1)

            def split_k(f):
                pool.wait_ge(k_sb, f + 1)
                if f >= 2:
                    pool.wait_ge(k_out, 16 * (f - 1))
                s, r, t = qk[:, f % 2, 1], resid[:, 1], k_parts[:, f % 2]
                link(pool.tensor_tensor(r, s, t[:, 0], ALU.subtract))
                pool.tensor_scalar(t[:, 1], r, 1.0, 0.0, ALU.mult, ALU.add).then_inc(k_split, 1)
                pool.wait_ge(k_split, 2 * f + 1)
                pool.tensor_tensor(t[:, 2], r, t[:, 1], ALU.subtract).then_inc(k_split, 1)

            def split_q(f):
                pool.wait_ge(q_sb, f + 1)
                pool.wait_ge(q_out, 16 * (f - 1))
                pool.wait_ge(q_split, f)
                s, r, t = qk[:, f % 2, 0], resid[:, 0], q_parts[:, f % 2]
                pool.tensor_tensor(r, s, t[:, 0], ALU.subtract).then_inc(q_rest, 1)
                pool.wait_ge(q_rest, 2 * f + 1)
                pool.tensor_scalar(t[:, 1], r, 1.0, 0.0, ALU.mult, ALU.add).then_inc(q_rest, 1)
                pool.wait_ge(q_rest, 2 * f + 2)
                pool.tensor_tensor(t[:, 2], r, t[:, 1], ALU.subtract).then_inc(q_split, 1)

            def split_x(f):
                pool.wait_ge(xnT_sb, f + 1)
                c, src = pair_cols(f - NP), inT[:, f % 2, :]
                link(pool.tensor_scalar(xn2T_hi[:, c], src, 1.0, 0.0, ALU.mult, ALU.add))
                pool.tensor_tensor(xn2T_lo[:, c], src, xn2T_hi[:, c].bitcast(F32), ALU.subtract)\
                    .then_inc(xsplit, 1)

            def split_h(p):
                pool.wait_ge(hT_sb, p + 1)
                c = pair_cols(p)
                link(pool.tensor_scalar(hT_hi[:, c], hT[:, p % 2], 1.0, 0.0, ALU.mult, ALU.add))
                pool.tensor_tensor(hT_lo[:, c], hT[:, p % 2], hT_hi[:, c].bitcast(F32), ALU.subtract)\
                    .then_inc(hsplit, 1)

            def split_weights(j):
                c = cols(j)
                if j == 0:
                    pool.wait_ge(ld_up, 32)
                for w, hi, lo in ((gate_w, gate_hi, gate_lo), (up_w, up_hi, up_lo)):
                    link(pool.tensor_scalar(hi[:, c], w[:, c], 1.0, 0.0, ALU.mult, ALU.add))
                    pool.tensor_tensor(lo[:, c], w[:, c], hi[:, c].bitcast(F32), ALU.subtract)\
                        .then_inc(wsplit, 1)

            def rstd2(b):
                pool.wait_ge(ln2_stats, b + 1)
                pool.tensor_tensor(rstd[:, 1, b:b + 1], ve[:, 1, b:b + 1], half_neg[:, b:b + 1], ALU.pow)\
                    .then_inc(ln2_rstd, 1)

            def rms(kind, t):
                link(pool.tensor_scalar(ms[:, kind, t], ss[:, kind, t], 1.0 / D, EPS, ALU.mult, ALU.add))
                return pool.tensor_tensor(rr[:, kind, t], ms[:, kind, t], half_neg[:, t], ALU.pow)

            def mask(i, q):
                pool.wait_ge(exp_done, NQ * i + q + 1)
                v = probs[:, i % 2, QH * P * q:QH * P * (q + 1)].rearrange("p (h q) -> p h q", h=QH)
                pool.affine_select(out=v, in_=v, compare_op=ALU.is_ge, fill=0.0, base=0,
                                   pattern=[[0, QH], [1, P]], channel_multiplier=-1).then_inc(masked, 1)

            def more_constants():
                link(pool.memset(ident_bf[:, :], 0.0))
                pool.affine_select(out=ident_bf[:, :], in_=ident_bf[:, :], compare_op=ALU.not_equal, fill=1.0,
                                   base=0, pattern=[[-1, P]], channel_multiplier=1).then_inc(consts, 1)
                link(pool.memset(causal_bf[:, :], 0.0))
                pool.affine_select(out=causal_bf[:, :], in_=causal_bf[:, :], compare_op=ALU.is_ge, fill=MASKED,
                                   base=0, pattern=[[-1, P]], channel_multiplier=1).then_inc(consts, 1)
                link(pool.memset(before[:, :, :], 1.0))
                pool.affine_select(out=before[:, :, :], in_=before[:, :, :], compare_op=ALU.is_gt, fill=0.0,
                                   base=0, pattern=[[1, NE], [-1, NE]], channel_multiplier=0).then_inc(consts, 1)

            def add_bo(p):
                if p == 0:
                    pool.wait_ge(ld_rows, 16)
                pool.wait_ge(ln1_ready, 2 * p + 2)
                for b in (2 * p, 2 * p + 1):
                    pool.tensor_tensor(x_sb[:, b, :], x_sb[:, b, :], rows["bo"][:, :], ALU.add)\
                        .then_inc(xbo_ready, 1)

            def rstd_a(i):
                pool.wait_ge(ss_a, i - B + 1)
                rms(0, slice(i - B, i - B + 1)).then_inc(rr_a, 1)

            def add_x2(i):
                pool.wait_ge(h_ready, i - B + 1)
                pool.tensor_tensor(xh[:, i - B, :], x2[:, i - B, :], hh[:, i - B, :], ALU.add).then_inc(xh_ready, 1)

            rstd1(0)
            rstd1(1)
            split_k(0)
            rstd1(2)
            rstd1(3)
            split_k(1)
            more_constants()
            add_bo(0)
            add_bo(3)
            add_bo(2)
            add_bo(1)
            for n in range(SLOTS):
                at(split_x, self_front_of(n - 1))
                at(mask, self_at(n - 2), 1)
                at(add_x2, self_at(n - 6))
                at(mask, self_at(n - 2), 2)
                at(rstd_a, self_at(n - 4))
                at(split_weights, WEIGHTS.get((n, 0)))
                at(split_k, front_of(n))
                at(rstd2, cross_at(n - 4))
                at(split_weights, WEIGHTS.get((n, 1)))
                at(split_weights, WEIGHTS.get((n, 2)))
                at(mask, self_at(n - 2), 3)
                at(split_h, hfront_of(n))
                at(mask, self_at(n - 1), 0)
            for c in range(NC):
                pool.wait_ge(ss_f, 4 * (c + 1))
                rms(1, slice(4 * c, 4 * c + 4)).then_inc(rr_f, 1)
                for t in range(0, 4, 2):
                    pool.wait_ge(ss_m, 4 * c + t + 2)
                    rms(2, slice(4 * c + t, 4 * c + t + 2)).then_inc(rr_m, 1)

        @block.scalar
        def _(act):
            act.dma_start(pa_sb[:, :], proj_a).then_inc(ld_pa, 16)
            act.dma_start(rows_sb[:, :, :].rearrange("p r d -> p (r d)"),
                          bass.AP(tensor=row_vectors.tensor, offset=row_vectors.offset,
                                  ap=[[0, P], [1, len(ROWS) * D]])).then_inc(ld_rows, 16)
            act.dma_start(pb_sb[:, :], proj_b).then_inc(ld_pb, 16)

            def evac_xnT(f):
                act.wait_ge(xnT_ps, f + 1)
                if f >= 2:
                    act.wait_ge(q_ps, f - 1)
                if f >= NP + 2:
                    act.wait_ge(v_ps, f - 1)
                    act.wait_ge(xsplit, f - NP - 1)
                act.copy(inT[:, f % 2, :], f_ps[:, 0:2 * P]).then_inc(xnT_sb, 1)

            def evac_part(f, n, src, bias, parts):
                if f < NP:
                    act.activation(qk[:, f % 2, n], src, ACT.Identity, bias=bias)
                    return act.activation(parts, src, ACT.Identity, bias=bias)
                act.copy(qk[:, f % 2, n], src)
                return act.copy(parts, src)

            def evac_k(f):
                act.wait_ge(k_ps if f < 2 else q_ps, f + 1)
                if f >= 2:
                    act.wait_ge(k_split, 2 * (f - 1))
                    act.wait_ge(k_wrap, f - 1)
                    act.wait_ge(k_out, 16 * (f - 1))
                evac_part(f, 1, front_k_ps(f), bk_sb, k_parts[:, f % 2, 0]).then_inc(k_sb, 1)

            def evac_q(f):
                act.wait_ge(q_ps, f + 1)
                if f >= 2:
                    act.wait_ge(q_split, f - 1)
                    act.wait_ge(q_out, 16 * (f - 1))
                evac_part(f, 0, f_ps[:, 0:2 * P], bq_sb, q_parts[:, f % 2, 0]).then_inc(q_sb, 1)

            def evac_v(f):
                act.wait_ge(v_ps, f + 1)
                b = 2 * (f - NP)
                act.copy(logits[:, b:b + 2, :].rearrange("p b e -> p (b e)"), f_ps[:, 2 * P:2 * P + 2 * NE])
                act.copy(v_aug[:, b:b + 2, :, 0:DK],
                         f_ps[:, 0:2 * P].rearrange("p (b h d) -> p b h d", b=2, h=H)).then_inc(v_ready, 1)

            def exps(i, q):
                act.wait_ge(sk_ready, NQ * i + q + 1)
                if i >= 2:
                    act.wait_ge(pv_done, NQ * (i - 1))
                act.activation(probs[:, i % 2, QH * P * q:QH * P * (q + 1)], s_kq[:, bank(q)], ACT.Exp,
                               scale=SCALE).then_inc(exp_done, 1)

            def take_maxrow(i):
                act.wait_ge(maxT_ready, i + 1)
                if i >= 2:
                    act.wait_ge(maxrow_in[i % 2], 16 * (i // 2))
                act.copy(maxrow[:, i % 2, :], m_ps[0:2 * H, 0:P]).then_inc(maxrow_ready, 1)

            def evac_o(i):
                act.wait_ge(pv_done, NQ * (i + 1))
                if i >= 2:
                    act.wait_ge(oT_ready, 2 * (i - 1))
                act.copy(o_sb[:, i % 2, :], o_ps[:, :]).then_inc(o_out, 1)

            def evac_onT(i):
                act.wait_ge(onT_ready, i + 1)
                if i >= 2:
                    act.wait_ge(wo_ready, i - 1)
                act.copy(o_normT[:, i % 2, :], m_ps[:, 0:P]).then_inc(onT_sb, 1)

            def attn_out(i):
                b = i - B
                act.wait_ge(wo_ready, i + 1)
                if b >= 2:
                    act.wait_ge(awn_done, b - 1)
                act.copy(aw[:, i % 2, :], m_ps[:, 0:P]).then_inc(wo_read, 1)
                act.wait_ge(wo_read, i + 1)
                act.activation(junk[:, :], aw[:, i % 2, :], ACT.Square, accum_out=ss[:, 0, b:b + 1])\
                    .then_inc(ss_a, 1)
                act.wait_ge(ss_a, b + 1)

            def evac_hT(p):
                act.wait_ge(hT_psr, p + 1)
                if p >= 2:
                    act.wait_ge(hsplit, p - 1)
                act.copy(hT[:, p % 2, :], f_ps[:, 0:2 * P]).then_inc(hT_sb, 1)

            def route_exp(c):
                act.wait_ge(rt_shift, c + 1)
                act.activation(rt[:, 4 + c].rearrange("p t e -> p (t e)"),
                               rt[:, 2 + c].rearrange("p t e -> p (t e)"), ACT.Exp).then_inc(rt_exp, 1)

            def silu(J):
                act.wait_ge(up_ready, J + 1)
                if J >= 2:
                    act.wait_ge(g_ready, J - 1)
                act.activation(sil[:, J % 2, :], hu_ps[J % 2][:, 0:4 * P], ACT.Silu).then_inc(silu_done, 1)

            def square(kind, src, done, c, t):
                if 4 * c + t:
                    act.wait_ge(done, 4 * c + t)
                act.activation(junk[:, :], src[:, t, :], ACT.Square,
                               accum_out=ss[:, kind, 4 * c + t:4 * c + t + 1]).then_inc(done, 1)

            def moe_squares(c):
                act.wait_ge(ss_f, 4 * (c + 1))
                for t in range(4):
                    act.wait_ge(acc_step, 4 * (NE * (c + 1) - 1) + t + 1)
                    square(2, moe, ss_m, c, t)

            def ff_block(J):
                c, j = divmod(J, NJ)
                silu(J)
                if c and j == 1:
                    moe_squares(c - 1)
                if j == ND + 1:
                    act.wait_ge(dense_ready, c + 1)
                    if c:
                        act.wait_ge(y1_mul, 4 * c)
                    act.copy(f_sb[:, :, :].rearrange("p t d -> p (t d)"), d_ps[:, :]).then_inc(dense_sb, 1)
                    act.wait_ge(dense_sb, c + 1)
                    act.wait_ge(*((ss_m, 4 * c) if c else (ss_a, B)))
                    for t in range(4):
                        square(1, f_sb, ss_f, c, t)

            evac_xnT(0)
            evac_k(0)
            evac_q(0)
            evac_k(1)
            evac_xnT(1)
            evac_q(1)
            for n in range(SLOTS):
                at(evac_hT, hfront_of(n - 1))
                at(take_maxrow, item_at(n - 1))
                at(exps, item_at(n - 2), 0)
                at(evac_xnT, front_of(n))
                at(exps, item_at(n - 2), 1)
                at(evac_o, item_at(n - 3))
                at(evac_onT, item_at(n - 4))
                at(ff_block, early(ACT_EARLY, n, 0))
                at(evac_k, front_of(n))
                at(route_exp, router_of(n - 1))
                at(exps, item_at(n - 2), 2)
                at(evac_v, self_front_of(n - 1))
                at(evac_q, front_of(n))
                at(attn_out, self_at(n - 4))
                at(exps, item_at(n - 2), 3)
                at(ff_block, early(ACT_EARLY, n, 1))
            for J in range(len(ACT_EARLY), NC * NJ):
                ff_block(J)
            moe_squares(NC - 1)

        @block.tensor
        def _(pe):
            def need(sems, count):
                for s in sems:
                    pe.wait_ge(s, count)

            def front_in(f):
                if f >= 1:
                    pe.wait_ge(q_sb, f)
                if f > NP:
                    pe.wait_ge(v_ready, f)
                src = xn if f < NP else xn2
                pe.wait_ge(ln1_ready if f < NP else ln2_ready, 2 * (f % NP) + 2)
                for t in range(2):
                    mm = pe.transpose(f_ps[:, cols(t)], src[:, 2 * (f % NP) + t, :], ident[:, :])
                mm.then_inc(xnT_ps, 1)

            def front_k(f):
                if f == 0:
                    need([ld_pa, ld_ctx[0]], 16)
                if f == 1:
                    pe.wait_ge(k_sb, 1)
                if f == 2:
                    pe.wait_ge(ld_ctx[1], 16)
                if f >= 2:
                    pe.wait_ge(xnT_sb, f + 1)
                w, src = (wts["wkT"], ctxT_sb[:, pair_cols(f)]) if f < NP else (wts["fwk"], inT[:, f % 2, :])
                pe.matmul(front_k_ps(f), w[:, :], src, start=True, stop=True).then_inc(k_ps, 1)

            def front_q(f):
                pe.wait_ge(xnT_sb, f + 1)
                w = wts["wqT"] if f < NP else wts["fwq"]
                pe.matmul(f_ps[:, 0:2 * P], w[:, :], inT[:, f % 2, :], start=True, stop=True).then_inc(q_ps, 1)

            def front_v(f):
                if f == 0:
                    pe.wait_ge(ld_pb, 16)
                if f == 2:
                    pe.wait_ge(ld_ctx[1], 16)
                if 1 <= f < NP:
                    pe.wait_ge(v_ready, f)
                if f >= NP:
                    pe.wait_ge(q_sb, f + 1)
                o = front_v_ps(f)
                for t in range(2):
                    src = ctxT_sb[:, cols(2 * f + t)] if f < NP else inT[:, f % 2, cols(t)]
                    w = wts["wvT"] if f < NP else wts["fwv"]
                    mm = pe.matmul(o[:, cols(t)], src, w[:, :], start=True, stop=True)
                    if f >= NP:
                        mm = pe.matmul(o[:, 2 * P + NE * t:2 * P + NE * (t + 1)], src,
                                       router_sb[:, :], start=True, stop=True)
                mm.then_inc(v_ps, 1)

            def scores_for_max(i, q):
                u = NQ * i + q
                if q == 0 and i % 2 == 0:
                    pe.wait_ge(stack[i // 2], 16 * 2 * TERMS)
                if u >= 2:
                    pe.wait_ge(max_done, u - 1)
                p, c = in_stack(i % B)
                causal = i >= B
                o = s_qk[:, bank(q)].rearrange("p (h k) -> p h k", h=QH)
                if causal:
                    pe.matmul(o, ident_bf[:, :],
                              causal_bf[:, :].rearrange("p (a k) -> p a k", a=1).broadcast_to([P, QH, P]),
                              start=True, stop=False, skip_group_check=True)
                for n in range(QH):
                    h = QH * q + n
                    mm = pe.matmul(o[:, n], q_stack[0:SROWS, p, h, c], k_stack[0:SROWS, p, h, c],
                                   start=not causal, stop=True, skip_group_check=causal)
                mm.then_inc(sq_ready, 1)

            m_read = [(v_ready, NP)]

            def max_transpose(i):
                pe.wait_ge(neg_split, i + 1)
                pe.wait_ge(*m_read.pop())
                m_read.append((maxrow_ready, i + 1))
                pe.matmul(m_ps[0:2 * H, 0:P], neg_parts[:, i % 2].rearrange("p t h -> p (t h)"), ident_bf[:, :],
                          start=True, stop=True).then_inc(maxT_ready, 1)

            def scores_for_exp(i, q):
                u = NQ * i + q
                if u == 0:
                    pe.wait_ge(k_ones, 16)
                if q == 0:
                    pe.wait_ge(maxrow_in[i % 2], 16 * (i // 2 + 1))
                if u >= 2:
                    pe.wait_ge(exp_done, u - 1)
                p, c = in_stack(i % B)
                o = s_kq[:, bank(q)]
                for n in range(QH):
                    h = QH * q + n
                    mm = pe.matmul(o[:, cols(n)], k_stack[0:SROWS + 2, p, h, c], q_stack[0:SROWS + 2, p, h, c],
                                   start=True, stop=True)
                mm.then_inc(sk_ready, 1)

            def probs_v(i, q):
                b, u = i % B, NQ * i + q
                if u == 0:
                    pe.wait_ge(ones_set, 2)
                if q == 0:
                    pe.wait_ge(v_ready, i // 2 + 1)
                if q == 0 and i >= 1:
                    pe.wait_ge(o_out, i)
                if i >= B:
                    pe.wait_ge(masked, u - NQ * B + 1)
                else:
                    pe.wait_ge(exp_done, u + 1)
                for n in range(QH):
                    h = QH * q + n
                    mm = pe.matmul(o_ps[32 * n:32 * n + DK + 1, cols(q)], v_aug[:, b, h, :],
                                   probs[:, i % 2, cols(h)], start=True, stop=True)
                mm.then_inc(pv_done, 1)

            def o_transpose(i, half):
                pe.wait_ge(o_out, i + 1)
                if i == 0:
                    pe.wait_ge(k_sb, 2)
                if i >= 1:
                    pe.wait_ge(on_ready, i)
                for g in (2 * half, 2 * half + 1):
                    mm = pe.transpose(oT_ps[:, cols(g)], o_sb[:, i % 2, cols(g)], ident[:, :])
                mm.then_inc(oT_ready, 1)

            def on_transpose(i):
                pe.wait_ge(on_ready, i + 1)
                pe.wait_ge(*m_read.pop())
                m_read.append((onT_sb, i + 1))
                pe.transpose(m_ps[:, 0:P], o_norm[:, i % 2, :], ident[:, :]).then_inc(onT_ready, 1)

            def project_o(i):
                pe.wait_ge(onT_sb, i + 1)
                if m_read[-1][0] is not onT_sb:
                    pe.wait_ge(*m_read[-1])
                m_read.pop()
                m_read.append((wo_read, i + 1))
                pe.matmul(m_ps[:, 0:P], o_normT[:, i % 2, :], (wts["woT"] if i < B else wts["fwo"])[:, :],
                          start=True, stop=True).then_inc(wo_ready, 1)

            def h_transpose(p):
                pe.wait_ge(v_ready, 2 * NP)
                if p >= 1:
                    pe.wait_ge(hT_sb, p)
                pe.wait_ge(h_ready, 2 * p + 2)
                for t in range(2):
                    mm = pe.transpose(f_ps[:, cols(t)], hh[:, 2 * p + t, :], ident[:, :])
                mm.then_inc(hT_psr, 1)

            pe.wait_ge(consts, 1)
            front_in(0)
            front_k(0)
            front_q(0)
            front_v(0)
            front_k(1)
            front_in(1)
            front_q(1)
            front_v(1)
            front_v(2)
            front_v(3)
            pe.wait_ge(consts, 3)
            def up(J):
                c, j = divmod(J, NJ)
                if j == 0:
                    pe.wait_ge(hsplit, 2 * (c + 1))
                    pe.wait_ge(xsplit, 2 * (c + 1))
                if J < 2:
                    pe.wait_ge((max_done, exp_done)[J], NQ * NI)
                    pe.wait_ge(wsplit, 2 * NJ)
                else:
                    pe.wait_ge(g_ready, J - 1)
                hi, lo = (hT_hi, hT_lo) if j < ND else (xn2T_hi, xn2T_lo)
                t = slice(4 * P * c, 4 * P * (c + 1))
                for n, (w_hi, w_lo) in enumerate(((gate_hi, gate_lo), (up_hi, up_lo))):
                    o = hu_ps[J % 2][:, 4 * P * n:4 * P * (n + 1)]
                    pe.matmul(o, w_hi[:, cols(j)], hi[:, t], start=True, stop=False)
                    pe.matmul(o, w_hi[:, cols(j)], lo[:, t], start=False, stop=False)
                    mm = pe.matmul(o, w_lo[:, cols(j)], hi[:, t], start=False, stop=True)
                mm.then_inc(up_ready, 1)

            def down_dense(c):
                pe.wait_ge(g_ready, NJ * c + ND)
                if c == 0:
                    pe.wait_ge(ld_down, 16)
                    pe.wait_ge(o_out, NI)
                else:
                    pe.wait_ge(dense_sb, c)
                for t in range(4):
                    for j in range(ND):
                        mm = pe.matmul(d_ps[:, cols(t)], g_dense[:, j, cols(t)], down_w[:, j, :],
                                       start=(j == 0), stop=(j == ND - 1))
                mm.then_inc(dense_ready, 1)

            def down_expert(c, e):
                k = NE * c + e
                pe.wait_ge(g_ready, NJ * c + ND + e + 1)
                if k < 2:
                    pe.wait_ge((on_ready, wo_read)[k], NI)
                else:
                    pe.wait_ge(acc_step, 4 * (k - 1))
                if k == LAST:
                    pe.wait_ge(hT_sb, NP)
                for t in range(4):
                    mm = pe.matmul(e_out(k, t), g_exp[:, k % 2, cols(t)], down_w[:, ND + e, :],
                                   start=True, stop=True)
                    if t % 2:
                        mm.then_inc(down_ready, 1)

            def ff_block(J):
                c, j = divmod(J, NJ)
                up(J)
                if c and j == 0:
                    down_expert(c - 1, NE - 1)
                if j == ND:
                    down_dense(c)
                if j > ND:
                    down_expert(c, j - ND - 1)

            for n in range(SLOTS):
                at(scores_for_max, item_at(n), 0)
                at(max_transpose, item_at(n - 1))
                at(scores_for_exp, item_at(n - 2), 0)
                at(scores_for_max, item_at(n), 1)
                at(front_in, front_of(n))
                at(front_v, self_front_of(n - 1))
                at(scores_for_exp, item_at(n - 2), 1)
                at(on_transpose, item_at(n - 4))
                at(probs_v, item_at(n - 3), 3)
                at(scores_for_max, item_at(n), 2)
                at(ff_block, early(PE_EARLY, n, 0))
                at(front_k, front_of(n))
                at(front_q, front_of(n))
                at(scores_for_exp, item_at(n - 2), 2)
                at(scores_for_max, item_at(n), 3)
                at(ff_block, early(PE_EARLY, n, 1))
                at(o_transpose, item_at(n - 3), 0)
                at(project_o, item_at(n - 4))
                at(o_transpose, item_at(n - 3), 1)
                at(scores_for_exp, item_at(n - 2), 3)
                at(h_transpose, hfront_of(n))
                at(probs_v, item_at(n - 2), 0)
                at(ff_block, early(PE_EARLY, n, 2))
                at(probs_v, item_at(n - 2), 1)
                at(probs_v, item_at(n - 2), 2)
            for J in range(len(PE_EARLY), NC * NJ):
                ff_block(J)
            down_expert(NC - 1, NE - 1)

        @block.vector
        def _(dve):
            chain = [0]

            def link(ins):
                chain[0] += 1
                ins.then_inc(dve_chain, 1)
                dve.wait_ge(dve_chain, chain[0])

            def ln1_stats(p):
                dve.wait_ge(ld_x[min(p, 1)], 16)
                for b in (2 * p, 2 * p + 1):
                    link(dve.bn_stats(stats[:, 0, b, :], x_sb[:, b, :]))
                    dve.bn_aggr(mv[:, 0, b, :], stats[:, 0, b, :]).then_inc(ln_stats, 1)

            def ln1_apply(p):
                dve.wait_ge(ln_rstd, p + 1)
                for b in (2 * p, 2 * p + 1):
                    dve.tensor_scalar(xn[:, b, :], x_sb[:, b, :], mv[:, 0, b, 0:1], rstd[:, 0, b:b + 1],
                                      ALU.subtract, ALU.mult).then_inc(ln1_ready, 1)

            def split_q(f, step):
                s, r, t = qk[:, f % 2, 0], resid[:, 0], q_parts[:, f % 2]
                if step == 0:
                    dve.wait_ge(q_sb, f + 1)
                    if f >= 2:
                        dve.wait_ge(q_out, 16 * (f - 1))
                    if f >= 1:
                        dve.wait_ge(q_split, f)
                    dve.tensor_tensor(r, s, t[:, 0], ALU.subtract).then_inc(q_rest, 1)
                if step == 1:
                    dve.wait_ge(q_rest, 2 * f + 1)
                    dve.tensor_copy(t[:, 1], r).then_inc(q_rest, 1)
                if step == 2:
                    dve.wait_ge(q_rest, 2 * f + 2)
                    dve.tensor_tensor(t[:, 2], r, t[:, 1], ALU.subtract).then_inc(q_split, 1)

            def wrap_k(f):
                dve.wait_ge(k_split, 2 * f + 1)
                if f >= 2:
                    dve.wait_ge(k_out, 16 * (f - 1))
                dve.tensor_copy(k_parts[:, f % 2, TERMS:], k_parts[:, f % 2, 0:TERMS - 1]).then_inc(k_wrap, 1)

            def take_v(f):
                dve.wait_ge(v_ps, f + 1)
                b = 2 * (f % NP)
                src = front_v_ps(f)[:, 0:2 * P].rearrange("p (b h d) -> p b h d", b=2, h=H)
                dst = v_aug[:, b:b + 2, :, 0:DK]
                if f == 0:
                    dve.wait_ge(ld_rows, 16)
                for t in range(2):
                    ins = dve.tensor_tensor(dst[:, t], src[:, t],
                                            rows["bv"][:, :].rearrange("p (h d) -> p h d", h=H), ALU.add)
                ins.then_inc(v_ready, 1)

            def maxima(i, q):
                dve.wait_ge(sq_ready, NQ * i + q + 1)
                dve.tensor_reduce(negmax[:, i % 2, QH * q:QH * (q + 1)],
                                  s_qk[:, bank(q)].rearrange("p (h k) -> p h k", h=QH), AX_X, ALU.max,
                                  negate=True).then_inc(max_done, 1)

            def split_max(i, part):
                if part == 0:
                    dve.wait_ge(max_done, NQ * (i + 1))
                    if i >= 2:
                        dve.wait_ge(maxT_ready, i - 1)
                    dve.tensor_copy(neg_parts[:, i % 2, 0, :], negmax[:, i % 2, :]).then_inc(neg_hi, 1)
                else:
                    dve.wait_ge(neg_hi, i + 1)
                    dve.tensor_tensor(neg_parts[:, i % 2, 1, :], negmax[:, i % 2, :], neg_parts[:, i % 2, 0, :],
                                      ALU.subtract).then_inc(neg_split, 1)

            def reciprocal(i):
                dve.wait_ge(oT_ready, 2 * (i + 1))
                v = oT_ps[:, :].rearrange("p (h d) -> p h d", h=H)
                dve.reciprocal(rsum[:, i % 2, :], v[:, :, DK]).then_inc(rec_done, 1)

            def normalise(i):
                if i >= 2:
                    dve.wait_ge(onT_ready, i - 1)
                v = oT_ps[:, :].rearrange("p (h d) -> p h d", h=H)
                dve.wait_ge(rec_done, i + 1)
                dve.tensor_tensor(o_norm[:, i % 2, :].rearrange("p (h d) -> p h d", h=H), v[:, :, 0:DK],
                                  rsum[:, i % 2, :].rearrange("p (h a) -> p h a", a=1).broadcast_to([P, H, DK]),
                                  ALU.mult).then_inc(on_ready, 1)

            def residual(b):
                dve.wait_ge(wo_ready, b + 1)
                dve.wait_ge(xbo_ready, b + 1)
                dve.tensor_tensor(x2[:, b, :], m_ps[:, 0:P], x_sb[:, b, :], ALU.add).then_inc(wo_read, 1)

            def ln2_stats_step(b, step):
                if step == 0:
                    dve.wait_ge(wo_read, b + 1)
                    dve.bn_stats(stats[:, 1, b, :], x2[:, b, :]).then_inc(st2, 1)
                if step == 1:
                    dve.wait_ge(st2, 2 * b + 1)
                    dve.bn_aggr(mv[:, 1, b, :], stats[:, 1, b, :]).then_inc(st2, 1)
                if step == 2:
                    dve.wait_ge(st2, 2 * b + 2)
                    dve.tensor_scalar(ve[:, 1, b:b + 1], mv[:, 1, b, 1:2], EPS, None, ALU.add)\
                        .then_inc(ln2_stats, 1)

            def ln2_apply(b):
                dve.wait_ge(ln2_rstd, b + 1)
                dve.tensor_scalar(xn2[:, b, :], x2[:, b, :], mv[:, 1, b, 0:1], rstd[:, 1, b:b + 1],
                                  ALU.subtract, ALU.mult).then_inc(ln2_ready, 1)

            def attn_scale(i):
                dve.wait_ge(wo_read, i + 1)
                dve.tensor_tensor(awn[:, i % 2, :], aw[:, i % 2, :], rows["attn_w"][:, :], ALU.mult)\
                    .then_inc(awn_done, 1)

            def attn_norm(i):
                b = i - B
                dve.wait_ge(awn_done, b + 1)
                dve.wait_ge(rr_a, b + 1)
                dve.scalar_tensor_tensor(out=hh[:, b, :], in0=awn[:, i % 2, :], scalar=rr[:, 0, b:b + 1],
                                         in1=xn2[:, b, :], op0=ALU.mult, op1=ALU.add).then_inc(h_ready, 1)

            def route_shift(c):
                lg = logits[:, 4 * c:4 * c + 4, :]
                dve.wait_ge(v_ready, NP + 2 * c + 2)
                if c:
                    dve.wait_ge(rt_shift, c)
                link(dve.tensor_reduce(rmx[:, 0, :], lg, AX_X, ALU.max))
                dve.tensor_tensor(rt[:, 2 + c], lg, wide(rmx[:, 0, :]), ALU.subtract).then_inc(rt_shift, 1)

            def wide(v):
                return v.rearrange("p (t a) -> p t a", a=1).broadcast_to([P, 4, NE])

            def route_gates(c):
                dve.wait_ge(rt_exp, c + 1)
                if c:
                    dve.wait_ge(gates_ready, c)
                dve.wait_ge(consts, 4)
                link(dve.tensor_reduce(rmx[:, 1, :], rt[:, 4 + c], AX_X, ALU.add))
                link(dve.reciprocal(rmx[:, 0, :], rmx[:, 1, :]))
                link(dve.tensor_tensor(rt[:, 0], rt[:, 4 + c], wide(rmx[:, 0, :]), ALU.mult))
                other = rt[:, 0].rearrange("p t (a e) -> p t a e", a=1).broadcast_to([P, 4, NE, NE])
                own = rt[:, 0].rearrange("p t (e a) -> p t e a", a=1).broadcast_to([P, 4, NE, NE])
                earlier = before[:, :, :].rearrange("p (a e) g -> p a e g", a=1).broadcast_to([P, 4, NE, NE])
                dve.tensor_tensor(cmp[:, 0], other, own, ALU.is_gt)
                link(dve.tensor_tensor(cmp[:, 1], other, own, ALU.is_equal))
                link(dve.tensor_tensor(cmp[:, 1], cmp[:, 1], earlier, ALU.mult))
                link(dve.tensor_tensor(cmp[:, 0], cmp[:, 0], cmp[:, 1], ALU.add))
                link(dve.tensor_reduce(rt[:, 1], cmp[:, 0], AX_X, ALU.add))
                dve.scalar_tensor_tensor(out=gates[:, 4 * c:4 * c + 4, :].rearrange("p t e -> p (t e)"),
                                         in0=rt[:, 1].rearrange("p t e -> p (t e)"), scalar=1.5,
                                         in1=rt[:, 0].rearrange("p t e -> p (t e)"),
                                         op0=ALU.is_lt, op1=ALU.mult).then_inc(gates_ready, 1)

            def gated(J):
                c, j = divmod(J, NJ)
                dve.wait_ge(silu_done, J + 1)
                if j < ND:
                    if c:
                        dve.wait_ge(dense_ready, c)
                    else:
                        dve.wait_ge(pv_done, NQ * (NI - 1))
                    dst = g_dense[:, j, :]
                else:
                    k = NE * c + j - ND
                    if k >= 2:
                        dve.wait_ge(down_ready, 2 * (k - 1))
                    else:
                        dve.wait_ge(pv_done, NQ * NI)
                    dst = g_exp[:, k % 2, :]
                dve.tensor_tensor(dst, sil[:, J % 2, :], hu_ps[J % 2][:, 4 * P:8 * P], ALU.mult)\
                    .then_inc(g_ready, 1)

            def add_expert(c, e):
                k = NE * c + e
                if k < LAST:
                    dve.wait_ge(down_ready, 2 * (k + 1))
                if e == 0:
                    dve.wait_ge(gates_ready, c + 1)
                if e == 0 and c:
                    dve.wait_ge(y2_ready, 4 * c)
                for t in range(4):
                    if k == LAST:
                        dve.wait_ge(down_ready, 2 * k + t // 2 + 1)
                    g = gates[:, 4 * c + t, e:e + 1]
                    src = e_out(k, t)
                    if e == 0:
                        dve.tensor_scalar(moe[:, t, :], src, g, None, ALU.mult).then_inc(acc_step, 1)
                    else:
                        dve.wait_ge(acc_step, 4 * (k - 1) + t + 1)
                        dve.scalar_tensor_tensor(out=moe[:, t, :], in0=src, scalar=g, in1=moe[:, t, :],
                                                 op0=ALU.mult, op1=ALU.add).then_inc(acc_step, 1)

            def finish(c):
                for t in range(4):
                    dve.wait_ge(acc_step, 4 * (NE * (c + 1) - 1) + t + 1)
                    dve.tensor_tensor(y2[:, t, :], moe[:, t, :], rows["moe_w"][:, :], ALU.mult)\
                        .then_inc(y2_ready, 1)
                for t in range(4):
                    b = 4 * c + t
                    dve.wait_ge(y2_ready, b + 1)
                    dve.wait_ge(rr_m, 2 * c + t // 2 + 1)
                    dve.wait_ge(y1_ready, b + 1)
                    dve.scalar_tensor_tensor(out=y_out[:, b, :], in0=y2[:, t, :], scalar=rr[:, 2, b:b + 1],
                                             in1=y1[:, t, :], op0=ALU.mult, op1=ALU.add).then_inc(y_ready, 1)

            def ff_block(J):
                c, j = divmod(J, NJ)
                gated(J)
                if c and j == 0:
                    add_expert(c - 1, NE - 1)
                if c and j == ND:
                    finish(c - 1)
                if j > ND:
                    add_expert(c, j - ND - 1)
                if j == ND + 4:
                    if c == 0:
                        dve.wait_ge(xh_ready, B)
                    dve.wait_ge(ss_f, 4 * (c + 1))
                    if c:
                        dve.wait_ge(y_ready, 4 * c)
                    for t in range(4):
                        dve.tensor_tensor(y1[:, t, :], f_sb[:, t, :], rows["ff_w"][:, :], ALU.mult)\
                            .then_inc(y1_mul, 1)
                if j == ND + 5:
                    dve.wait_ge(rr_f, c + 1)
                    for t in range(4):
                        b = 4 * c + t
                        dve.wait_ge(y1_mul, b + 1)
                        dve.scalar_tensor_tensor(out=y1[:, t, :], in0=y1[:, t, :], scalar=rr[:, 1, b:b + 1],
                                                 in1=xh[:, b, :], op0=ALU.mult, op1=ALU.add).then_inc(y1_ready, 1)

            def set_ones_row():
                dve.memset(ones_row[:, :], 1.0).then_inc(row_set, 1)

            def set_ones_columns():
                dve.memset(v_aug[:, :, :, DK:DK + 1], 1.0).then_inc(ones_set, 1)

            def clear_o():
                dve.memset(o_ps[:, :], 0.0).then_inc(ones_set, 1)

            ln1_stats(0)
            set_ones_row()
            ln1_apply(0)
            set_ones_columns()
            ln1_stats(1)
            ln1_stats(2)
            ln1_stats(3)
            split_q(0, 0)
            split_q(0, 1)
            split_q(0, 2)
            wrap_k(0)
            ln1_apply(1)
            take_v(0)
            clear_o()
            split_q(1, 0)
            split_q(1, 1)
            split_q(1, 2)
            take_v(1)
            ln1_apply(2)
            take_v(2)
            wrap_k(1)
            ln1_apply(3)
            take_v(3)
            for n in range(SLOTS):
                at(split_q, front_of(n - 1), 1)
                at(ff_block, early(DVE_EARLY, n, 0))
                at(ln2_apply, cross_at(n - 5, odd=1))
                at(maxima, item_at(n), 0)
                at(attn_norm, self_at(n - 5))
                at(ff_block, early(DVE_EARLY, n, 1))
                at(split_q, front_of(n - 1), 2)
                at(wrap_k, front_of(n - 1))
                at(maxima, item_at(n), 1)
                at(maxima, item_at(n), 2)
                at(maxima, item_at(n), 3)
                at(residual, cross_at(n - 4))
                at(ln2_stats_step, cross_at(n - 4), 0)
                at(split_max, item_at(n), 0)
                at(ln2_stats_step, cross_at(n - 4), 1)
                at(reciprocal, item_at(n - 3))
                at(ln2_stats_step, cross_at(n - 4), 2)
                at(split_max, item_at(n), 1)
                at(route_shift, router_of(n))
                at(attn_scale, self_at(n - 4))
                at(ln2_apply, cross_at(n - 5, odd=0))
                at(split_q, front_of(n), 0)
                at(normalise, item_at(n - 3))
                at(route_gates, {NI + GAP: 0, NI + GAP + 1: 1}.get(n))
            for J in range(len(DVE_EARLY), NC * NJ):
                ff_block(J)
            add_expert(NC - 1, NE - 1)
            finish(NC - 1)


def kernel(**inputs):
    import numpy as _np
    import concourse.bacc as _bacc
    from concourse import mybir as _mybir
    from concourse.bass_utils import run_bass_kernel_spmd as _run

    nc = _bacc.Bacc("TRN2", target_bir_lowering=False, num_devices=1)
    a = {name: _np.asarray(v) for name, v in inputs.items()}
    xa = {n: a["L0_xattn_" + n] for n in ("Wq", "bq", "Wk", "bk", "Wv", "bv", "Wo", "bo")}
    fa = {n[len("L0_ffn_"):]: v for n, v in a.items() if n.startswith("L0_ffn_")}

    def blocks(w):
        return w.reshape(-1, EH, D).transpose(1, 0, 2).reshape(EH, -1)

    def beside(w):
        return w.transpose(1, 0, 2).reshape(D, -1)

    side = lambda *parts: _np.concatenate(parts, axis=1)
    arrays = {
        "in_x": a["x"],
        "in_ctxT": a["ctx_1024"].transpose(2, 0, 1).reshape(D, -1),
        "in_proj_a": side(xa["Wq"].T, xa["Wk"].T, xa["bq"][:, None], xa["bk"][:, None]),
        "in_proj_b": side(xa["Wv"].T, xa["Wo"].T, fa["wq"], fa["wk"], fa["wv"], fa["wo"], fa["router_w"]),
        "in_rows": _np.concatenate([xa["bv"], xa["bo"], fa["attn_norm_w"], fa["ff_norm_w"], fa["moe_norm_w"]]),
        "in_gate": side(fa["w1"], beside(fa["ew1"])),
        "in_up": side(fa["w3"], beside(fa["ew3"])),
        "in_down": side(blocks(fa["w2"]), blocks(fa["ew2"])),
    }
    arrays = {name: _np.ascontiguousarray(v) for name, v in arrays.items()}
    args = [nc.dram_tensor(name, v.shape, _mybir.dt.from_np(v.dtype), kind="ExternalInput").ap()
            for name, v in arrays.items()]
    y = nc.dram_tensor("out_0", a["x"].shape, _mybir.dt.float32, kind="ExternalOutput").ap()
    build(nc, *args, y)
    r = _run(nc, [arrays], core_ids=[0])
    return r.results[0]["out_0"]
```
